# Optimizing a Trainium2 kernel written in Bass

```python
import numpy as np
import jax
import jax.numpy as jnp

def _softmax(x, axis=-1):
    return jax.nn.softmax(x, axis=axis)

def _gelu(x):
    return jax.nn.gelu(x, approximate=True)

def _silu(x):
    return jax.nn.silu(x)

def _sigmoid(x):
    return jax.nn.sigmoid(x)

def _layernorm(x, axis=-1, eps=1e-05):
    m = jnp.mean(x, axis=axis, keepdims=True)
    v = jnp.var(x, axis=axis, keepdims=True)
    return (x - m) / jnp.sqrt(v + eps)

def _scatter_add(tgt, idx, src, axis=0):
    return tgt.at[idx].add(src)

def _segment_sum(src, seg, n):
    return jax.ops.segment_sum(src, seg, n)
kernel_name = 'mk_gnn_preln_d4_gnn_r32_8cfa77'

def setup_inputs(seed: int=0):
    np.random.seed(seed)
    _w = jnp.asarray

    def _rec_inputs():
        import jax
        import jax.numpy as jnp
        _gk = jax.random.key(seed)
        x = -0.0001006 + 1 * jax.random.normal(jax.random.fold_in(_gk, 1), (3125, 48), jnp.float32)
        _s = jax.random.randint(jax.random.fold_in(_gk, 2), (50000,), 0, 3125, jnp.int32)
        _d = jax.random.randint(jax.random.fold_in(_gk, 3), (50000,), 0, 3125, jnp.int32)
        _loop = jnp.arange(3125, dtype=jnp.int32)
        src = jnp.concatenate([_s, _d, _loop])
        dst = jnp.concatenate([_d, _s, _loop])
        _o = jnp.argsort(dst, stable=True)
        src = src[_o]
        dst = dst[_o]
        edge_attr_40 = jax.random.uniform(jax.random.fold_in(_gk, 13), (103125, 40), jnp.float32, 0.0, 1)
        edge_type_8 = jax.random.randint(jax.random.fold_in(_gk, 15), (103125,), 0, 8, jnp.int32)
        edge_weight = jax.random.uniform(jax.random.fold_in(_gk, 16), (103125,), jnp.float32, 0.0, 6.99999)
        edge_weight1 = jax.random.uniform(jax.random.fold_in(_gk, 17), (103125, 1), jnp.float32, 0.0, 1)
        node_type_119 = jax.random.randint(jax.random.fold_in(_gk, 18), (3125,), 0, 119, jnp.int32)
        node_vec = jax.random.uniform(jax.random.fold_in(_gk, 19), (3125,), jnp.float32, 0.0, 1.49999)
        return (x, src, dst, edge_attr_40, edge_type_8, edge_weight, edge_weight1, node_type_119, node_vec)
    x, src, dst, edge_attr_40, edge_type_8, edge_weight, edge_weight1, node_type_119, node_vec = _rec_inputs()

    def _L0_gnn_setup():
        import jax, jax.numpy as jnp
        import numpy as np
        N_NODES = 3125
        N_EDGES = 50000
        IN_F = 48
        HID_F = 48
        OUT_F = 48

        def _sage_mean(x, src, dst, W_self, W_neigh, b, n_nodes):
            deg = jax.ops.segment_sum(jnp.ones((src.shape[0],), x.dtype), dst, num_segments=n_nodes)
            agg = jax.ops.segment_sum(x[src], dst, num_segments=n_nodes)
            h_neigh = agg / jnp.maximum(deg, 1.0)[:, None]
            return x @ W_self + h_neigh @ W_neigh + b
        key = jax.random.key(seed)
        ks = jax.random.split(key, 9)
        features = jax.random.normal(ks[0], (N_NODES, IN_F), dtype=jnp.float32)
        src = jax.random.randint(ks[1], (N_EDGES,), 0, N_NODES)
        dst = jax.random.randint(ks[2], (N_EDGES,), 0, N_NODES)
        s_in = 1.0 / np.sqrt(IN_F)
        s_hid = 1.0 / np.sqrt(HID_F)
        return {'features': features, 'src': src, 'dst': dst, 'W_self1': jax.random.normal(ks[3], (IN_F, HID_F), jnp.float32) * s_in, 'W_neigh1': jax.random.normal(ks[4], (IN_F, HID_F), jnp.float32) * s_in, 'b1': jnp.zeros((HID_F,), jnp.float32), 'W_self2': jax.random.normal(ks[5], (HID_F, OUT_F), jnp.float32) * s_hid, 'W_neigh2': jax.random.normal(ks[6], (HID_F, OUT_F), jnp.float32) * s_hid, 'b2': jnp.zeros((OUT_F,), jnp.float32)}
    _L0_gnn_all = _L0_gnn_setup()
    _L0_gnn_in = {k: v for k, v in _L0_gnn_all.items() if k in ('W_self1', 'W_neigh1', 'b1', 'W_self2', 'W_neigh2', 'b2')}
    del _L0_gnn_all

    def _L1_gnn_setup():
        import jax, jax.numpy as jnp
        import numpy as np
        N_NODES = 50000
        N_EDGES = 50000
        IN_FEAT = 48
        OUT_FEAT = 48
        NUM_RELS = 8
        key = jax.random.key(seed)
        ks = jax.random.split(key, 9)
        s1 = float(np.sqrt(2.0) * np.sqrt(6.0 / (IN_FEAT + IN_FEAT)))
        s2 = float(np.sqrt(2.0) * np.sqrt(6.0 / (IN_FEAT + OUT_FEAT)))
        return {'inputs': jax.random.normal(ks[0], (N_NODES, IN_FEAT), dtype=jnp.float32), 'norm': jax.random.uniform(ks[1], (N_EDGES, 1), dtype=jnp.float32), 'weight1': jax.random.uniform(ks[2], (NUM_RELS, IN_FEAT, IN_FEAT), jnp.float32, -s1, s1), 'weight2': jax.random.uniform(ks[3], (NUM_RELS, IN_FEAT, OUT_FEAT), jnp.float32, -s2, s2), 'bias1': jax.random.normal(ks[4], (IN_FEAT,), dtype=jnp.float32) * 0.1, 'bias2': jax.random.normal(ks[5], (OUT_FEAT,), dtype=jnp.float32) * 0.1, 'src': jax.random.randint(ks[6], (N_EDGES,), 0, N_NODES, dtype=jnp.int64) if jax.config.jax_enable_x64 else jax.random.randint(ks[6], (N_EDGES,), 0, N_NODES).astype(jnp.int32), 'dst': jax.random.randint(ks[7], (N_EDGES,), 0, N_NODES).astype(jnp.int32), 'rel_type': jax.random.randint(ks[8], (N_EDGES,), 0, NUM_RELS).astype(jnp.int32)}
    _L1_gnn_all = _L1_gnn_setup()
    _L1_gnn_in = {k: v for k, v in _L1_gnn_all.items() if k in ('weight1', 'weight2', 'bias1', 'bias2')}
    del _L1_gnn_all

    def _L2_gnn_setup():
        import jax, jax.numpy as jnp
        import numpy as np
        CUTOFF = 6.0
        LN_EPS = 1e-05
        key = jax.random.key(seed)
        ks = jax.random.split(key, 16)
        N, E, H, R, NEL, G = (50000, 25000, 48, 40, 119, 32)
        inp = {'h': jax.random.normal(ks[0], (N, H), jnp.float32), 'edge_index': jax.random.randint(ks[1], (2, E), 0, N, jnp.int64), 'edge_attr': jax.random.uniform(ks[2], (E, R), jnp.float32), 'distances': jax.random.uniform(ks[3], (E,), jnp.float32) * 7.0, 'atom_z': jax.random.randint(ks[4], (N,), 0, NEL, jnp.int64), 'node_mult': jax.random.uniform(ks[5], (N,), jnp.float32) + 0.5, 'batch': jnp.zeros((N,), jnp.int64), 'W1': jax.random.normal(ks[6], (H, R), jnp.float32) / np.sqrt(R), 'b1': jax.random.normal(ks[7], (H,), jnp.float32) * 0.01, 'W2': jax.random.normal(ks[8], (H, H), jnp.float32) / np.sqrt(H), 'b2': jax.random.normal(ks[9], (H,), jnp.float32) * 0.01, 'emb': jax.random.normal(ks[10], (NEL, G), jnp.float32) * 0.01, 'adaptW': jax.random.normal(ks[11], (G, G), jnp.float32) * 0.01, 'gamma': jnp.ones((H,), jnp.float32), 'beta': jnp.zeros((H,), jnp.float32)}
        return inp
    _L2_gnn_all = _L2_gnn_setup()
    _L2_gnn_in = {k: v for k, v in _L2_gnn_all.items() if k in ('W1', 'b1', 'W2', 'b2', 'emb', 'adaptW', 'gamma', 'beta')}
    del _L2_gnn_all

    def _L3_gnn_setup():
        import jax, jax.numpy as jnp
        import numpy as np
        N_NODES = 3125
        N_EDGES = 50000
        N_CLASSES = 48
        key = jax.random.key(seed)
        k1, k2, k3, k4 = jax.random.split(key, 4)
        soft_label = jax.random.normal(k1, (N_NODES, N_CLASSES), dtype=jnp.float32)
        e = jax.random.normal(k2, (N_EDGES, 1), dtype=jnp.float32)
        src = jax.random.randint(k3, (N_EDGES,), 0, N_NODES)
        dst = jax.random.randint(k4, (N_EDGES,), 0, N_NODES)
        return {'soft_label': soft_label, 'e': e, 'src': src, 'dst': dst}
    _L3_gnn_all = _L3_gnn_setup()
    _L3_gnn_in = {k: v for k, v in _L3_gnn_all.items() if k in ()}
    del _L3_gnn_all
    return {'x': x, 'src': src, 'dst': dst, 'edge_attr_40': edge_attr_40, 'edge_type_8': edge_type_8, 'edge_weight': edge_weight, 'edge_weight1': edge_weight1, 'node_type_119': node_type_119, 'node_vec': node_vec, 'L0_gnn_W_self1': _L0_gnn_in['W_self1'], 'L0_gnn_W_neigh1': _L0_gnn_in['W_neigh1'], 'L0_gnn_b1': _L0_gnn_in['b1'], 'L0_gnn_W_self2': _L0_gnn_in['W_self2'], 'L0_gnn_W_neigh2': _L0_gnn_in['W_neigh2'], 'L0_gnn_b2': _L0_gnn_in['b2'], 'L1_gnn_weight1': _L1_gnn_in['weight1'], 'L1_gnn_weight2': _L1_gnn_in['weight2'], 'L1_gnn_bias1': _L1_gnn_in['bias1'], 'L1_gnn_bias2': _L1_gnn_in['bias2'], 'L2_gnn_W1': _L2_gnn_in['W1'], 'L2_gnn_b1': _L2_gnn_in['b1'], 'L2_gnn_W2': _L2_gnn_in['W2'], 'L2_gnn_b2': _L2_gnn_in['b2'], 'L2_gnn_emb': _L2_gnn_in['emb'], 'L2_gnn_adaptW': _L2_gnn_in['adaptW'], 'L2_gnn_gamma': _L2_gnn_in['gamma'], 'L2_gnn_beta': _L2_gnn_in['beta']}

def reference(x, src, dst, edge_attr_40, edge_type_8, edge_weight, edge_weight1, node_type_119, node_vec, L0_gnn_W_self1, L0_gnn_W_neigh1, L0_gnn_b1, L0_gnn_W_self2, L0_gnn_W_neigh2, L0_gnn_b2, L1_gnn_weight1, L1_gnn_weight2, L1_gnn_bias1, L1_gnn_bias2, L2_gnn_W1, L2_gnn_b1, L2_gnn_W2, L2_gnn_b2, L2_gnn_emb, L2_gnn_adaptW, L2_gnn_gamma, L2_gnn_beta):
    import jax
    import jax.numpy as jnp

    def _L0_gnn_ref(features, src, dst, W_self1, W_neigh1, b1, W_self2, W_neigh2, b2):
        import jax, jax.numpy as jnp
        import numpy as np
        N_NODES = 3125
        N_EDGES = 50000
        IN_F = 48
        HID_F = 48
        OUT_F = 48

        def _sage_mean(x, src, dst, W_self, W_neigh, b, n_nodes):
            deg = jax.ops.segment_sum(jnp.ones((src.shape[0],), x.dtype), dst, num_segments=n_nodes)
            agg = jax.ops.segment_sum(x[src], dst, num_segments=n_nodes)
            h_neigh = agg / jnp.maximum(deg, 1.0)[:, None]
            return x @ W_self + h_neigh @ W_neigh + b
        n = features.shape[0]
        h = jax.nn.relu(_sage_mean(features, src, dst, W_self1, W_neigh1, b1, n))
        out = _sage_mean(h, src, dst, W_self2, W_neigh2, b2, n)
        return out

    def _L1_gnn_ref(inputs, norm, weight1, weight2, bias1, bias2, src, dst, rel_type):
        import jax, jax.numpy as jnp
        import numpy as np
        N_NODES = 50000
        N_EDGES = 50000
        IN_FEAT = 48
        OUT_FEAT = 48
        NUM_RELS = 8
        h1 = jax.nn.relu(jnp.einsum('ni,rij->nrj', inputs, weight1) + bias1)
        h2 = jnp.einsum('nrj,rjo->nro', h1, weight2)
        msg = h2[src, rel_type] * norm
        agg = jax.ops.segment_sum(msg, dst, num_segments=inputs.shape[0])
        return jax.nn.relu(agg + bias2)

    def _L2_gnn_ref(h, edge_index, edge_attr, distances, atom_z, node_mult, batch, W1, b1, W2, b2, emb, adaptW, gamma, beta):
        import jax, jax.numpy as jnp
        import numpy as np
        CUTOFF = 6.0
        LN_EPS = 1e-05
        src, dst = (edge_index[0], edge_index[1])
        N = h.shape[0]
        gate = jax.nn.silu(edge_attr @ W1.T + b1) @ W2.T + b2
        ei = emb[atom_z[src]]
        ej = emb[atom_z[dst]]
        adapt_logit = jnp.sum(ei * (ej @ adaptW.T), axis=-1, keepdims=True)
        gate = gate + adapt_logit
        cw = jnp.where(distances < CUTOFF, 0.5 * (jnp.cos(jnp.pi * distances / CUTOFF) + 1.0), 0.0)
        mj = node_mult[dst]
        msg = gate * h[dst] * (cw * mj)[:, None]
        agg = jax.ops.segment_sum(msg, src, num_segments=N)
        tot = jax.ops.segment_sum(mj, src, num_segments=N)
        agg = agg / jnp.clip(tot, 1e-08, None)[:, None]
        x = h + agg
        mu = jnp.mean(x, axis=-1, keepdims=True)
        var = jnp.mean(jnp.square(x - mu), axis=-1, keepdims=True)
        return (x - mu) / jnp.sqrt(var + LN_EPS) * gamma + beta

    def _L3_gnn_ref(soft_label, e, src, dst):
        import jax, jax.numpy as jnp
        import numpy as np
        N_NODES = 3125
        N_EDGES = 50000
        N_CLASSES = 48
        N = soft_label.shape[0]
        logits = e[:, 0]
        seg_max = jax.ops.segment_max(logits, dst, num_segments=N)
        seg_max = jnp.where(jnp.isfinite(seg_max), seg_max, 0.0)
        ex = jnp.exp(logits - seg_max[dst])
        seg_sum = jax.ops.segment_sum(ex, dst, num_segments=N)
        a = ex / seg_sum[dst]
        msg = soft_label[src] * a[:, None]
        rst = jax.ops.segment_sum(msg, dst, num_segments=N)
        return jax.nn.elu(rst)
    edge_index = jnp.stack([src, dst])
    batch0 = jnp.zeros((3125,), jnp.int32)
    h = jnp.maximum(_layernorm(x, axis=-1), 0.0)
    x = x + _L0_gnn_ref(h, src, dst, L0_gnn_W_self1, L0_gnn_W_neigh1, L0_gnn_b1, L0_gnn_W_self2, L0_gnn_W_neigh2, L0_gnn_b2)
    h = jnp.maximum(_layernorm(x, axis=-1), 0.0)
    x = x + _L1_gnn_ref(h, edge_weight1, L1_gnn_weight1, L1_gnn_weight2, L1_gnn_bias1, L1_gnn_bias2, src, dst, edge_type_8)
    h = jnp.maximum(_layernorm(x, axis=-1), 0.0)
    x = x + _L2_gnn_ref(h, edge_index, edge_attr_40, edge_weight, node_type_119, node_vec, batch0, L2_gnn_W1, L2_gnn_b1, L2_gnn_W2, L2_gnn_b2, L2_gnn_emb, L2_gnn_adaptW, L2_gnn_gamma, L2_gnn_beta)
    h = jnp.maximum(_layernorm(x, axis=-1), 0.0)
    x = x + _L3_gnn_ref(h, edge_weight1, src, dst)
    return x

_drawn_inputs = setup_inputs


def setup_inputs(seed=0):
    import zlib

    import numpy as np

    out = dict(_drawn_inputs(seed))
    spreads = {'L0_gnn_b1': (0.0, 0.1),
     'L0_gnn_b2': (0.0, 0.1),
     'L2_gnn_gamma': (1.0, 0.2),
     'L2_gnn_beta': (0.0, 0.387)}
    factors = {'edge_attr_40': 8.0,
     'edge_weight': 8.0,
     'node_vec': 8.0,
     'L1_gnn_bias2': 3.077,
     'L2_gnn_b1': 178.15,
     'L2_gnn_W2': 2.79,
     'L2_gnn_b2': 200.0,
     'L2_gnn_emb': 64.0,
     'L2_gnn_adaptW': 64.0}
    for name, (base, spread) in spreads.items():
        noise = np.random.default_rng([zlib.crc32(name.encode()), seed]).standard_normal(out[name].shape)
        drawn = base * np.exp(spread * noise) if base else spread * noise
        out[name] = jnp.asarray(drawn.astype(out[name].dtype))
    for name, factor in factors.items():
        out[name] = (out[name] * factor).astype(out[name].dtype)
    return out
```

```python
from contextlib import ExitStack

import concourse.bass as bass
from concourse import mybir

P = 128
ALU = mybir.AluOpType
ACT = mybir.ActivationFunctionType
AX_X = mybir.AxisListType.X
F32 = mybir.dt.float32
BF16 = mybir.dt.bfloat16
I32 = mybir.dt.int32

N = 3125
E = 103125
F = 48
ATTR = 40
RELS = 8
GDIM = 32
KINDS = 119

TILES = -(-N // P)
LAST = N - (TILES - 1) * P
NODES = TILES * P
U = 8
GROUP = P * U
PAIRS = -(-E // (2 * GROUP))
GROUPS = 2 * PAIRS
CHUNKS = GROUPS * U
FULL = E // GROUP
TAIL = E - FULL * GROUP
TAIL_P, TAIL_U = divmod(TAIL, U)
BUCKETS = TILES + 1
TURNS = -(-(-(-E // P) + TILES) // (2 * U))
SLOTS = TURNS * 2 * U
PAD_CHUNKS = -(-(CHUNKS * P - E) // P)
ROW = SLOTS + PAD_CHUNKS
SLOT_COLS = -(-SLOTS // P)
META1 = 4
META2 = 52
W0 = 64
WQ = 96
CUTOFF = 6.0
EPS = 1e-5
BIG = 1e38
NG = 5
NTURNS = TILES // NG
HALF_PI = 1.5707963267948966
assert FULL == GROUPS - 2 and N % P and TILES % NG == 0 and E // P + TILES <= SLOTS


class Steps:

    def __init__(self, eng, sem, start=0):
        self.eng, self.sem, self.start, self.n = eng, sem, start, 0

    def done(self, ins):
        self.n += 1
        ins.then_inc(self.sem, 1)
        self.eng.wait_ge(self.sem, self.start + self.n)


class Phase(ExitStack):

    def __init__(self, nc):
        super().__init__()
        self.nc, self.sems = nc, []

    def semaphore(self, name):
        self.sems.append(self.nc.alloc_semaphore(name))
        return self.sems[-1]

    def __exit__(self, *error):
        self.nc.clear_and_free_semaphores(self.sems)
        self.nc.all_engine_barrier()
        return super().__exit__(*error)


def bc(ap, n):
    return ap.unsqueeze(len(ap.shape)).broadcast_to(list(ap.shape) + [n])


def mid(ap, n):
    return ap.unsqueeze(1).broadcast_to([ap.shape[0], n, ap.shape[1]])


def column(vector):
    return vector.rearrange("(p a) -> p a", a=1)


def row_of(vector):
    return vector.rearrange("(a f) -> a f", a=1)


def node_rows(dram, p0, p1, t0, t1):
    return dram[t0 * P:t1 * P, :].rearrange("(t p) f -> p t f", p=P)[p0:p1]


def put_table(eng, table, tile, words, sem):
    eng.dma_start(table.rearrange("(t p) w -> p t w", p=P)[:, :, 0:words], tile).then_inc(sem, 16)


def layernorm_relu(dve, act, s, x, h, tmp, stat, steps, ln_var, ln_std, turn, relu=True):
    if act is not None:
        act.wait_ge(ln_var, turn)
        act.activation(stat[:, 2, :], stat[:, 1, :], ACT.Sqrt, bias=s.eps[:, :], scale=1.0 / F).then_inc(ln_std, 1)
        return
    steps.done(dve.tensor_reduce(stat[:, 0, :], x, AX_X, ALU.add))
    steps.done(dve.tensor_scalar(stat[:, 0, :], stat[:, 0, :], 1.0 / F, None, ALU.mult))
    steps.done(dve.tensor_tensor(h, x, bc(stat[:, 0, :], F), ALU.subtract))
    steps.done(dve.tensor_tensor(tmp, h, h, ALU.mult))
    dve.tensor_reduce(stat[:, 1, :], tmp, AX_X, ALU.add).then_inc(ln_var, 1)
    dve.wait_ge(ln_std, turn)
    steps.done(dve.reciprocal(stat[:, 3, :], stat[:, 2, :]))
    steps.done(dve.tensor_tensor(h, h, bc(stat[:, 3, :], F), ALU.mult))
    if relu:
        steps.done(dve.tensor_scalar(h, h, 0.0, None, ALU.max))


class Store:
    pass


def setup_phase(nc, s, d):
    with Phase(nc) as ctx:
        sb = lambda n, shape, dt=F32: ctx.enter_context(nc.sbuf_tensor(n, shape, dt))
        sem = lambda n: ctx.semaphore(n)
        src_i = sb("src_i", [P, GROUPS, U], I32)
        dst_i = sb("dst_i", [P, GROUPS, U], I32)
        typ_i = sb("typ_i", [P, GROUPS, U], I32)
        dist = sb("dist", [P, GROUPS, U])
        w1 = sb("w1", [P, GROUPS, U])
        f_a = sb("f_a", [P, CHUNKS])
        f_b = sb("f_b", [P, CHUNKS])
        iota_i = sb("iota_i", [P, P], I32)
        lane_i = sb("lane_i", [P, 1], I32)
        iota_slot_i = sb("iota_slot_i", [P, SLOT_COLS], I32)
        tmp = sb("tmp", [P, TILES, F])
        emb_t = sb("emb_t", [GDIM, KINDS])
        emb = sb("emb", [KINDS, GDIM])
        adapt_t = sb("adapt_t", [GDIM, GDIM])
        adapt = sb("adapt", [GDIM, GDIM])
        emb_pq = sb("emb_pq", [KINDS, 2 * GDIM])
        kind_row = sb("kind_row", [P, NODES], I32)
        kind_f = sb("kind_f", [P, NODES])
        tr_ps = ctx.enter_context(nc.psum_tensor("tr_ps", [P, 512], F32))
        q_ps = ctx.enter_context(nc.psum_tensor("q_ps", [P, 512], F32))
        pq_ps = ctx.enter_context(nc.psum_tensor("pq_ps", [P, 4, 8, 64], F32))
        s_blank = sem("s_blank")
        s_edges = sem("s_edges")
        s_x = sem("s_x")
        s_small = sem("s_small")
        s_iota = sem("s_iota")
        s_const = sem("s_const")
        s_kind = sem("s_kind")
        s_kindf = sem("s_kindf")
        s_cos_in = sem("s_cos_in")
        s_cos = sem("s_cos")
        s_dve = sem("s_dve")
        s_var = sem("s_var")
        s_std = sem("s_std")
        s_tr = sem("s_tr")
        s_trc = sem("s_trc")
        s_q = sem("s_q")
        s_qc = sem("s_qc")
        s_pq = sem("s_pq")
        s_h = sem("s_h")
        s_out = sem("s_out")
        flat = lambda t: t[:, :, :].rearrange("p g u -> p (g u)")
        with nc.Block() as block:
            @block.sync
            def _(sp):
                sp.wait_ge(s_blank, 1)
                sp.dma_start(s.x[:, 0:TILES - 1, :], node_rows(d.x, 0, P, 0, TILES - 1)).then_inc(s_x, 16)
                sp.dma_start(s.x[0:LAST, TILES - 1, :], d.x[(TILES - 1) * P:N, :]).then_inc(s_x, 16)
                for dram, tile in ((d.dst, dst_i), (d.src, src_i), (d.edge_type_8, typ_i), (d.edge_weight, dist), (d.edge_weight1, w1)):
                    v = dram if len(dram.shape) == 1 else dram.rearrange("e a -> (e a)")
                    cut = FULL * GROUP + TAIL_P * U
                    sp.dma_start(tile[:, 0:FULL, :], v[0:FULL * GROUP].rearrange("(g p u) -> p g u", p=P, u=U)).then_inc(s_edges, 16)
                    sp.dma_start(tile[0:TAIL_P, FULL, :], v[FULL * GROUP:cut].rearrange("(p u) -> p u", u=U)).then_inc(s_edges, 16)
                    sp.dma_start(tile[TAIL_P:TAIL_P + 1, FULL, 0:TAIL_U], row_of(v[cut:E])).then_inc(s_edges, 16)
                sp.wait_ge(s_h, 1)
                put_table(sp, d.table, s.tab[:, :, 0:W0], W0, s_out)
                sp.wait_ge(s_out, 16)

            @block.scalar
            def _(act):
                act.dma_start(emb[:, :], d.L2_gnn_emb).then_inc(s_small, 16)
                act.dma_start(adapt[:, :], d.L2_gnn_adaptW).then_inc(s_small, 16)
                act.dma_start(kind_row[:, 0:N], row_of(d.node_type_119).broadcast_to([P, N])).then_inc(s_kind, 16)
                act.wait_ge(s_blank, 1)
                act.dma_start(s.nvec[:, 0:TILES - 1], d.node_vec[0:(TILES - 1) * P].rearrange("(t p) -> p t", p=P)).then_inc(s_small, 16)
                act.dma_start(s.nvec[0:LAST, TILES - 1:TILES], column(d.node_vec[(TILES - 1) * P:N])).then_inc(s_small, 16)
                layernorm_relu(None, act, s, None, None, None, s.stat, None, s_var, s_std, 1)
                act.wait_ge(s_cos_in, 1)
                act.activation(f_b[:, :], f_a[:, :], ACT.Sin, bias=s.half_pi[:, :], scale=-2.0 * HALF_PI / CUTOFF).then_inc(s_cos, 1)

            @block.gpsimd
            def _(pool):
                pool.iota(iota_i[:, :], [[1, P]], base=0, channel_multiplier=0).then_inc(s_iota, 1)
                pool.iota(lane_i[:, :], [[1, 1]], base=0, channel_multiplier=1).then_inc(s_iota, 1)
                pool.iota(iota_slot_i[:, :], [[P, SLOT_COLS]], base=0, channel_multiplier=1).then_inc(s_iota, 1)

            @block.tensor
            def _(pe):
                pe.wait_ge(s_const, 1)
                pe.wait_ge(s_small, 64)
                pe.transpose(tr_ps[0:GDIM, 0:KINDS], emb[:, :], s.ident[0:KINDS, 0:KINDS])
                pe.transpose(tr_ps[0:GDIM, P:P + GDIM], adapt[:, :], s.ident[0:GDIM, 0:GDIM]).then_inc(s_tr, 1)
                pe.wait_ge(s_trc, 2)
                pe.matmul(q_ps[0:KINDS, 0:GDIM], emb_t[:, :], adapt_t[:, :], start=True, stop=True).then_inc(s_q, 1)
                pe.wait_ge(s_kindf, 1)
                pe.wait_ge(s_qc, 2)
                for t in range(TILES):
                    last = pe.matmul(pq_ps[:, t // 8, t % 8, :], kind_f[0:KINDS, t * P:(t + 1) * P], emb_pq[:, :],
                                     start=True, stop=True)
                last.then_inc(s_pq, 1)

            @block.vector
            def _(dve):
                dve.memset(s.x[:, :, :], 0.0)
                dve.memset(s.nvec[:, :], 0.0)
                for tile, value in ((dst_i, NODES), (src_i, NODES), (typ_i, 0), (dist, 0.0), (w1, 0.0)):
                    last = dve.memset(tile[:, FULL:GROUPS, :], value)
                last.then_inc(s_blank, 1)
                dve.memset(s.tab[:, :, :], 1.0)
                dve.memset(s.eps[:, :], EPS)
                dve.memset(s.half_pi[:, :], HALF_PI)
                dve.memset(s.ones[:, :], 1.0)
                dve.memset(s.zeros[:, :], 0.0)
                dve.memset(s.zeros_b[:, :], 0.0)
                dve.memset(s.sentinel1[:, :, :], 0.0)
                last = dve.memset(s.sentinel2[:, :, :], 0.0)
                steps = Steps(dve, s_dve)
                steps.done(last)
                dve.memset(s.sentinel1[:, :, 2:3], -1.0)
                steps.done(dve.memset(s.sentinel2[:, :, F + 1:F + 2], -1.0))
                dve.wait_ge(s_iota, 3)
                dve.tensor_copy(s.lane[:, :], lane_i[:, :])
                dve.tensor_copy(s.iota_slot[:, :], iota_slot_i[:, :])
                steps.done(dve.tensor_copy(s.iota[:, :], iota_i[:, :]))
                dve.tensor_scalar(s.lower[:, :], s.iota[:, :], s.lane[:, 0:1], None, ALU.is_gt)
                dve.tensor_scalar(s.ident_b[:, :], s.iota[:, :], s.lane[:, 0:1], None, ALU.is_equal)
                dve.tensor_scalar(s.ident[:, :], s.iota[:, :], s.lane[:, 0:1], None, ALU.is_equal).then_inc(s_const, 1)

                dve.wait_ge(s_x, 32)
                layernorm_relu(dve, None, s, s.x[:, :, :], s.h[:, :, :], tmp[:, :, :], s.stat, steps, s_var, s_std, 1)
                dve.tensor_copy(s.tab[:, :, 0:F], s.h[:, :, :]).then_inc(s_h, 1)

                dve.wait_ge(s_tr, 1)
                dve.tensor_copy(emb_t[:, :], tr_ps[0:GDIM, 0:KINDS]).then_inc(s_trc, 1)
                dve.tensor_copy(adapt_t[:, :], tr_ps[0:GDIM, P:P + GDIM]).then_inc(s_trc, 1)
                dve.tensor_copy(emb_pq[:, 0:GDIM], emb[:, :]).then_inc(s_qc, 1)
                dve.wait_ge(s_q, 1)
                dve.tensor_copy(emb_pq[:, GDIM:], q_ps[0:KINDS, 0:GDIM]).then_inc(s_qc, 1)
                dve.wait_ge(s_kind, 16)
                steps.done(dve.memset(kind_row[:, N:NODES], 0))
                dve.tensor_scalar(kind_f[:, :], kind_row[:, :], s.lane[:, 0:1], None, ALU.is_equal).then_inc(s_kindf, 1)
                dve.wait_ge(s_pq, 1)
                for b in range(0, TILES, 8):
                    n = min(8, TILES - b)
                    dve.tensor_copy(s.pnode[:, b:b + n, :], pq_ps[:, b // 8, 0:n, 0:GDIM])
                    dve.tensor_copy(s.qnode[:, b:b + n, :], pq_ps[:, b // 8, 0:n, GDIM:])

                dve.wait_ge(s_edges, 15 * 16)
                dve.tensor_scalar(s.cell[:, :], flat(dst_i), 7, None, ALU.logical_shift_right)
                dve.tensor_copy(s.meta2[:, :, 0], flat(dst_i))
                steps.done(dve.tensor_copy(s.meta1[:, :, 0], flat(src_i)))
                dve.tensor_copy(s.meta1[:, :, 3], flat(w1))
                steps.done(dve.tensor_copy(s.tile_d[:, :], s.cell[:, :]))
                dve.tensor_scalar(s.cell[:, :], flat(src_i), 7, None, ALU.logical_shift_right)
                steps.done(dve.tensor_copy(f_a[:, :], flat(typ_i)))
                dve.scalar_tensor_tensor(s.meta1[:, :, 1], s.meta1[:, :, 0], float(RELS), f_a[:, :], ALU.mult, ALU.add)
                dve.scalar_tensor_tensor(s.meta1[:, :, 2], s.tile_d[:, :], -float(P), s.meta2[:, :, 0], ALU.mult, ALU.add)
                steps.done(dve.tensor_copy(s.tile_s[:, :], s.cell[:, :]))
                dve.scalar_tensor_tensor(s.meta2[:, :, 1], s.tile_s[:, :], -float(P), s.meta1[:, :, 0], ALU.mult, ALU.add)
                dve.memset(s.meta2[:, :, 3], 0.0)
                steps.done(dve.tensor_scalar(f_b[:, :], flat(dist), -1.0, None, ALU.mult))
                steps.done(dve.tensor_tensor(f_b[:, :], f_b[:, :], flat(dist), ALU.max))
                dve.tensor_scalar(f_a[:, :], f_b[:, :], CUTOFF, None, ALU.min).then_inc(s_cos_in, 1)
                dve.wait_ge(s_cos, 1)
                steps.done(dve.tensor_scalar(f_b[:, :], f_b[:, :], 0.5, 0.5, ALU.mult, ALU.add))
                dve.scalar_tensor_tensor(s.meta2[:, :, 2], flat(dist), CUTOFF, f_b[:, :], ALU.is_lt, ALU.mult)


def rank_phase(nc, s, key, rows, chunk_tile, chunk_tile_dram, name):
    with Phase(nc) as ctx:
        sb = lambda n, shape, dt=F32: ctx.enter_context(nc.sbuf_tensor(f"{name}_{n}", shape, dt))
        sem = lambda n: ctx.semaphore(f"{name}_{n}")
        match = sb("match", [P, CHUNKS])
        cum = sb("cum", [P, CHUNKS])
        term = sb("term", [P, CHUNKS])
        pos = sb("pos", [P, CHUNKS])
        none = sb("none", [P, CHUNKS])
        count = sb("count", [P, BUCKETS])
        base = sb("base", [P, BUCKETS])
        first = sb("first", [P, BUCKETS])
        small = sb("small", [P, BUCKETS])
        small_i = sb("small_i", [P, BUCKETS], I32)
        blank = sb("blank", [P, BUCKETS])
        cmp = sb("cmp", [P, SLOT_COLS, BUCKETS])
        tile_f = sb("tile_f", [P, SLOT_COLS])
        tile_i = sb("tile_i", [P, SLOT_COLS], I32)
        ps = ctx.enter_context(nc.psum_tensor(f"{name}_ps", [P, 2, BUCKETS], F32))
        s_step = sem("s_step")
        s_count = sem("s_count")
        s_sums = sem("s_sums")
        s_tile = sem("s_tile")
        s_out = sem("s_out")
        s_back = sem("s_back")
        A = 2
        with nc.Block() as block:
            @block.vector
            def _(dve):
                steps = Steps(dve, s_step)
                dve.memset(pos[:, :], 0.0)
                dve.memset(none[:, :], 0.0)
                steps.done(dve.memset(blank[:, :], 0.0))
                with dve.Fori(0, BUCKETS) as t:
                    turn = Steps(dve, s_step, t * A + 1)
                    turn.done(dve.tensor_scalar(match[:, :], key, s.iota[:, bass.ds(t, 1)], None, ALU.is_equal))
                    turn.done(dve.tensor_reduce(count[:, bass.ds(t, 1)], match[:, :], AX_X, ALU.add))
                steps.n = A * BUCKETS + 1
                dve.drain().then_inc(s_count, 1)
                dve.wait_ge(s_sums, 1)
                steps.done(dve.tensor_scalar(small[:, :], ps[:, 0, :], float(P - 1), None, ALU.add))
                steps.done(dve.tensor_copy(small_i[:, :], small[:, :]))
                steps.done(dve.tensor_scalar(small_i[:, :], small_i[:, :], 7, None, ALU.logical_shift_right))
                steps.done(dve.tensor_copy(small[:, :], small_i[:, :]))
                steps.done(dve.tensor_tensor_scan(first[:, :], small[:, :], blank[:, :], 0.0, ALU.add, ALU.add))
                steps.done(dve.tensor_tensor(first[:, :], first[:, :], small[:, :], ALU.subtract))
                steps.done(dve.memset(first[:, TILES:BUCKETS], float(SLOTS)))
                steps.done(dve.scalar_tensor_tensor(base[:, :], first[:, :], float(P), ps[:, 1, :], ALU.mult, ALU.add))
                steps.done(dve.tensor_scalar(base[:, :], base[:, :], 1.0, None, ALU.subtract))
                for j in range(SLOT_COLS):
                    last = dve.tensor_scalar(cmp[:, j, :], first[:, :], s.iota_slot[:, j:j + 1], None, ALU.is_le)
                steps.done(last)
                steps.done(dve.tensor_reduce(tile_f[:, :], cmp[:, :, 1:TILES], AX_X, ALU.add))
                dve.tensor_copy(tile_i[:, :], tile_f[:, :]).then_inc(s_tile, 1)
                at = steps.n
                with dve.Fori(0, BUCKETS) as t:
                    turn = Steps(dve, s_step, t * 4 + (1 + at))
                    turn.start = t * 4 + at
                    turn.done(dve.tensor_scalar(match[:, :], key, s.iota[:, bass.ds(t, 1)], None, ALU.is_equal))
                    turn.done(dve.tensor_tensor_scan(cum[:, :], match[:, :], none[:, :], 0.0, ALU.add, ALU.add))
                    turn.done(dve.scalar_tensor_tensor(term[:, :], cum[:, :], base[:, bass.ds(t, 1)], match[:, :], ALU.add, ALU.mult))
                    turn.done(dve.tensor_tensor(pos[:, :], pos[:, :], term[:, :], ALU.add))
                steps.n = at + 4 * BUCKETS
                steps.done(dve.tensor_copy(s.cell[:, :], pos[:, :]))
                steps.done(dve.tensor_scalar(rows[:, :], s.cell[:, :], P - 1, None, ALU.bitwise_and))
                steps.done(dve.tensor_scalar(s.cell[:, :], s.cell[:, :], 7, None, ALU.logical_shift_right))
                dve.tensor_copy(match[:, :], rows[:, :])
                steps.done(dve.tensor_copy(cum[:, :], s.cell[:, :]))
                steps.done(dve.scalar_tensor_tensor(term[:, :], match[:, :], float(ROW), cum[:, :], ALU.mult, ALU.add))
                dve.tensor_copy(rows[:, :], term[:, :])

            @block.tensor
            def _(pe):
                pe.wait_ge(s_count, 1)
                pe.matmul(ps[:, 0, :], s.ones[:, :], count[:, :], start=True, stop=True)
                pe.matmul(ps[:, 1, :], s.lower[:, :], count[:, :], start=True, stop=True).then_inc(s_sums, 1)

            @block.sync
            def _(sp):
                sp.wait_ge(s_tile, 1)
                sp.dma_start(chunk_tile_dram.rearrange("(j p) -> p j", p=P), tile_i[:, :]).then_inc(s_out, 16)
                sp.wait_ge(s_out, 16)
                if chunk_tile is not None:
                    sp.dma_start(chunk_tile, row_of(chunk_tile_dram[0:SLOTS]).broadcast_to([P, SLOTS])).then_inc(s_back, 16)
                    sp.wait_ge(s_back, 16)


def fill_phase(nc, s, d):
    with Phase(nc) as ctx:
        s_out = ctx.semaphore("fill_out")
        s_zero = ctx.semaphore("fill_zero")
        with nc.Block() as block:
            @block.sync
            def _(sp):
                sp.dma_start(d.zeros.rearrange("(p a) -> p a", p=P), s.zeros[:, 0:U * ATTR]).then_inc(s_zero, 16)
                n = 0
                for dram, tile in ((d.sorted1, s.sentinel1), (d.sorted2, s.sentinel2)):
                    v = dram.rearrange("(p k) w -> p k w", p=P)
                    step = tile.shape[1]
                    for k in range(0, SLOTS, step):
                        sp.dma_start(v[:, k:k + step, :], tile[:, :, :]).then_inc(s_out, 16)
                        n += 16
                sp.wait_ge(s_zero, 16)
                sp.wait_ge(s_out, n)


def sort_phase(nc, s, d):
    with Phase(nc) as ctx:
        sb = lambda n, shape, dt=F32: ctx.enter_context(nc.sbuf_tensor(n, shape, dt))
        sem = lambda n: ctx.semaphore(n)
        w1_raw = sb("w1_raw", [F, ATTR])
        w2_raw = sb("w2_raw", [F, F])
        w1_t = sb("w1_t", [ATTR, F])
        w2_t = sb("w2_t", [F, F])
        b1 = sb("b1c", [F, 1])
        b2 = sb("b2r", [P, F])
        attr = [sb(f"attr{h}", [P, U, ATTR]) for h in range(2)]
        attr_t = sb("attr_t", [ATTR, U * P])
        act_t = sb("act_t", [F, U * P])
        pay1 = [sb(f"pay1_{h}", [P, U, META1]) for h in range(2)]
        pay2 = [sb(f"pay2_{h}", [P, U, META2]) for h in range(2)]
        at1 = [sb(f"at1_{h}", [P, U], I32) for h in range(2)]
        at2 = [sb(f"at2_{h}", [P, U], I32) for h in range(2)]
        tr_ps = ctx.enter_context(nc.psum_tensor("attr_ps", [P, U * P], F32))
        z_ps = ctx.enter_context(nc.psum_tensor("z_ps", [P, U * P], F32))
        g_ps = ctx.enter_context(nc.psum_tensor("gate_ps", [P, U, 64], F32))
        s_w = sem("sort_w")
        s_wt = sem("sort_wt")
        s_wc = sem("sort_wc")
        s_zero = sem("sort_zero")
        s_tail = sem("sort_tail")
        s_attr = [sem(f"sort_attr{h}") for h in range(2)]
        s_turned = sem("sort_turned")
        s_attr_t = sem("sort_attr_t")
        s_z = sem("sort_z")
        s_act = sem("sort_act")
        s_gate = sem("sort_gate")
        s_gated = sem("sort_gated")
        s_staged = [sem(f"sort_staged{h}") for h in range(2)]
        s_go = sem("sort_go")
        s_pe_go = sem("sort_pe_go")
        s_sent = [sem(f"sort_sent{h}") for h in range(2)]
        with nc.Block() as block:
            @block.sync
            def _(sp):
                sp.dma_start(w1_raw[:, :], d.L2_gnn_W1).then_inc(s_w, 16)
                sp.dma_start(w2_raw[:, :], d.L2_gnn_W2).then_inc(s_w, 16)
                sp.dma_start(b1[:, :], column(d.L2_gnn_b1)).then_inc(s_w, 16)
                sp.dma_start(b2[:, :], row_of(d.L2_gnn_b2).broadcast_to([P, F])).then_inc(s_w, 16)
                sp.sem_inc(s_turned, 1)
                sp.sem_inc(s_turned, 1)
                with sp.Fori(0, PAIRS - 1) as i:
                    for h in range(2):
                        sp.wait_ge(s_turned, i * 2 + (h + 1))
                        sp.dma_start(attr[h][:, :, :], d.edge_attr_40[bass.ds(i * (2 * GROUP) + h * GROUP, GROUP), :].rearrange(
                            "(p u) f -> p u f", u=U)).then_inc(s_attr[h], 16)
                cut = FULL * GROUP + TAIL_P * U
                for h in range(2):
                    sp.wait_ge(s_turned, 2 * (PAIRS - 1) + h + 1)
                    ins = sp.dma_start(attr[h][:, :, :].rearrange("p u f -> p (u f)"), d.zeros.rearrange("(p a) -> p a", p=P))
                    if h == 0:
                        ins.then_inc(s_zero, 16)
                        sp.wait_ge(s_zero, 16)
                        sp.dma_start(attr[0][0:TAIL_P, :, :], d.edge_attr_40[FULL * GROUP:cut, :].rearrange("(p u) f -> p u f", u=U)).then_inc(s_tail, 16)
                        sp.wait_ge(s_tail, 16)
                        ins = sp.dma_start(attr[0][TAIL_P:TAIL_P + 1, 0:TAIL_U, :], d.edge_attr_40[cut:E, :].rearrange("(p u) f -> p u f", u=TAIL_U))
                    ins.then_inc(s_attr[h], 16)

            @block.tensor
            def _(pe):
                pe.wait_ge(s_w, 64)
                pe.transpose(tr_ps[0:ATTR, 0:F], w1_raw[:, :], s.ident[0:F, 0:F])
                pe.transpose(tr_ps[0:F, F:2 * F], w2_raw[:, :], s.ident[0:F, 0:F]).then_inc(s_wt, 1)
                pe.wait_ge(s_wc, 2)
                with pe.Fori(0, PAIRS) as i:
                    for h in range(2):
                        g = i * 2 + h
                        pe.wait_ge(s_attr[h], i * 16 + 16)
                        pe.wait_ge(s_attr_t, g + 1)
                        pe.sem_inc(s_pe_go, 1)
                        for u in range(U):
                            last = pe.transpose(tr_ps[0:ATTR, u * P:(u + 1) * P], attr[h][:, u, :], s.ident[:, :])
                        last.then_inc(s_turned, 1)
                        pe.wait_ge(s_attr_t, g + 2)
                        pe.wait_ge(s_act, g + 1)
                        pe.sem_inc(s_pe_go, 1)
                        for c in range(0, U * P, 512):
                            last = pe.matmul(z_ps[0:F, c:c + 512], w1_t[:, :], attr_t[:, c:c + 512], start=True, stop=True)
                        last.then_inc(s_z, 1)
                        pe.wait_ge(s_act, g + 2)
                        pe.wait_ge(s_gated, g + 1)
                        pe.sem_inc(s_pe_go, 1)
                        for u in range(U):
                            last = pe.matmul(g_ps[:, u, 0:F], act_t[:, u * P:(u + 1) * P], w2_t[:, :], start=True, stop=True)
                        last.then_inc(s_gate, 1)

            @block.scalar
            def _(act):
                act.sem_inc(s_attr_t, 1)
                act.sem_inc(s_act, 1)
                act.sem_inc(s_gate, 1)
                act.wait_ge(s_wt, 1)
                act.copy(w1_t[:, :], tr_ps[0:ATTR, 0:F]).then_inc(s_wc, 1)
                act.copy(w2_t[:, :], tr_ps[0:F, F:2 * F]).then_inc(s_wc, 1)
                act.sem_inc(s_z, 1)
                with act.Fori(0, PAIRS) as i:
                    for h in range(2):
                        g = i * 2 + h
                        act.wait_ge(s_sent[h], i * (32 * U) + 16)
                        act.copy(pay1[h][:, :, :], s.meta1[:, bass.ds(i * (2 * U) + h * U, U), :]).then_inc(s_staged[h], 1)
                        act.copy(pay2[h][:, :, F:META2], s.meta2[:, bass.ds(i * (2 * U) + h * U, U), :]).then_inc(s_staged[h], 1)
                        act.copy(at1[h][:, :], s.rows1[:, bass.ds(i * (2 * U) + h * U, U)]).then_inc(s_staged[h], 1)
                        act.copy(at2[h][:, :], s.rows2[:, bass.ds(i * (2 * U) + h * U, U)]).then_inc(s_staged[h], 1)
                        act.wait_ge(s_turned, g + 3)
                        act.wait_ge(s_z, g + 1)
                        act.copy(attr_t[:, :], tr_ps[0:ATTR, :]).then_inc(s_attr_t, 1)
                        act.wait_ge(s_z, g + 2)
                        act.wait_ge(s_gate, g + 1)
                        act.activation(act_t[:, :], z_ps[0:F, :], ACT.Silu, bias=b1[:, 0:1]).then_inc(s_act, 1)

            @block.vector
            def _(dve):
                dve.sem_inc(s_gated, 1)
                dve.wait_ge(s_w, 64)
                with dve.Fori(0, PAIRS) as i:
                    for h in range(2):
                        g = i * 2 + h
                        dve.wait_ge(s_sent[h], i * (32 * U) + 16)
                        dve.wait_ge(s_gate, g + 2)
                        dve.tensor_tensor(pay2[h][:, :, 0:F], g_ps[:, :, 0:F], mid(b2[:, :], U), ALU.add).then_inc(s_gated, 1)

            @block.gpsimd
            def _(pool):
                for h in range(2):
                    pool.dma_start(pay1[h][:, 0, :], d.zeros.rearrange("(p a) -> p a", p=P)[:, 0:META1]).then_inc(s_sent[h], 16)
                with pool.Fori(0, PAIRS) as i:
                    for h in range(2):
                        pool.wait_ge(s_staged[h], i * 4 + 4)
                        pool.sem_inc(s_go, 1)
                        for u in range(U):
                            pool.indirect_dma_start(d.sorted1, bass.IndirectOffsetOnAxis(ap=at1[h][:, u:u + 1], axis=0),
                                                    pay1[h][:, u, :], None).then_inc(s_sent[h], 16)
                        pool.wait_ge(s_gated, i * 2 + (h + 2))
                        pool.sem_inc(s_go, 1)
                        for u in range(U):
                            pool.indirect_dma_start(d.sorted2, bass.IndirectOffsetOnAxis(ap=at2[h][:, u:u + 1], axis=0),
                                                    pay2[h][:, u, :], None).then_inc(s_sent[h], 16)
                for h in range(2):
                    pool.wait_ge(s_sent[h], PAIRS * 32 * U + 16)


def reload_phase(nc, s, d):
    with Phase(nc) as ctx:
        s_in = ctx.semaphore("reload_in")
        with nc.Block() as block:
            @block.sync
            def _(sp):
                sp.dma_start(s.edge1[:, :, :], d.sorted1.rearrange("(p k) w -> p k w", p=P)[:, 0:SLOTS, :]).then_inc(s_in, 16)

            @block.vector
            def _(dve):
                dve.wait_ge(s_in, 16)
                dve.tensor_copy(s.lane1[:, :], s.edge1[:, :, 2])
                dve.tensor_copy(s.weight1[:, :], s.edge1[:, :, 3])
                dve.tensor_copy(s.chunk_tile[:, :], s.chunk_tile_i[:, :])


def edge_pass(nc, s, d, name, table, width, used, index, weight=None, find_max=False, join_max=False, edge_max=False):
    with Phase(nc) as ctx:
        sb = lambda n, shape, dt=F32: ctx.enter_context(nc.sbuf_tensor(f"{name}_{n}", shape, dt))
        sem = lambda n: ctx.semaphore(f"{name}_{n}")
        stage = [sb(f"stage{h}", [P, U], I32) for h in range(2)]
        rows = [sb(f"rows{h}", [P, U, width]) for h in range(2)]
        scaled = [sb(f"scaled{h}", [P, U, width]) for h in range(2)] if weight is not None else rows
        onehot = [sb(f"onehot{h}", [P, U, P]) for h in range(2)]
        masked = [sb(f"masked{h}", [P, U, P]) for h in range(2)]
        line = sb("line", [P, SLOTS])
        acc = ctx.enter_context(nc.psum_tensor(f"{name}_acc", [P, 32, 64], F32))
        side = [ctx.enter_context(nc.psum_tensor(f"{name}_side{h}", [P, U, P], F32)) for h in range(2)]
        s_staged = [sem(f"staged{h}") for h in range(2)]
        s_go = sem("go")
        s_rows = [sem(f"rows{h}") for h in range(2)]
        s_scaled = [sem(f"scaled{h}") for h in range(2)]
        s_onehot = [sem(f"onehot{h}") for h in range(2)]
        s_masked = [sem(f"masked{h}") for h in range(2)]
        s_side = [sem(f"side{h}") for h in range(2)]
        s_side_read = [sem(f"side_read{h}") for h in range(2)]
        s_added = [sem(f"added{h}") for h in range(2)]
        s_step = sem("step")
        s_sum = sem("sum")
        extra = find_max or edge_max
        ready = s_scaled if weight is not None else s_rows
        per = 1 if weight is not None else 16 * U
        with nc.Block() as block:
            @block.scalar
            def _(act):
                for h in range(2):
                    act.sem_inc(s_added[h], 1)
                with act.Fori(0, TURNS) as i:
                    for h in range(2):
                        act.wait_ge(s_added[h], i + 1)
                        act.copy(stage[h][:, :], index[:, bass.ds(i * (2 * U) + h * U, U)]).then_inc(s_staged[h], 1)

            @block.gpsimd
            def _(pool):
                with pool.Fori(0, TURNS) as i:
                    for h in range(2):
                        pool.wait_ge(s_staged[h], i + 1)
                        pool.sem_inc(s_go, 1)
                        for u in range(U):
                            pool.indirect_dma_start(rows[h][:, u, :], None, table,
                                                    bass.IndirectOffsetOnAxis(ap=stage[h][:, u:u + 1], axis=0)).then_inc(s_rows[h], 16)

            @block.vector
            def _(dve):
                with dve.Fori(0, TURNS) as i:
                    steps_per = 2 * (1 if find_max else 0) + 2 * (1 if edge_max else 0) + (3 if join_max else 0)
                    turn = Steps(dve, s_step, i * steps_per)
                    for h in range(2):
                        k = i * (2 * U) + h * U
                        dve.wait_ge(s_added[h], i + 1)
                        for u in range(U):
                            last = dve.tensor_scalar(onehot[h][:, u, :], s.iota[:, :], s.lane1[:, bass.ds(k + u, 1)], None, ALU.is_equal)
                        last.then_inc(s_onehot[h], 1)
                        if weight is not None:
                            dve.wait_ge(s_rows[h], i * (16 * U) + 16 * U)
                            dve.tensor_tensor(scaled[h][:, :, :], rows[h][:, :, :], bc(weight[:, bass.ds(k, U)], width),
                                              ALU.mult).then_inc(s_scaled[h], 1)
                        if find_max:
                            dve.wait_ge(s_onehot[h], i + 1)
                            turn.done(dve.tensor_scalar(masked[h][:, :, :], onehot[h][:, :, :], BIG, -BIG, ALU.mult, ALU.add))
                            dve.tensor_tensor(masked[h][:, :, :], masked[h][:, :, :], bc(s.weight1[:, bass.ds(k, U)], P),
                                              ALU.add).then_inc(s_masked[h], 1)
                            dve.wait_ge(s_side[h], i + 1)
                            dve.tensor_reduce(s.top[:, bass.ds(k, U)], side[h][:, :, :], AX_X, ALU.max).then_inc(s_side_read[h], 1)
                        if edge_max:
                            dve.wait_ge(s_side[h], i + 1)
                            dve.wait_ge(s_onehot[h], i + 1)
                            dve.tensor_tensor(masked[h][:, :, :], onehot[h][:, :, :], side[h][:, :, :], ALU.mult).then_inc(s_side_read[h], 1)
                            dve.wait_ge(s_side_read[h], i + 2)
                            turn.done(dve.tensor_reduce(s.edge_top[:, bass.ds(k, U)], masked[h][:, :, :], AX_X, ALU.add))
                    if join_max:
                        turn.done(dve.tensor_scalar(line[:, :], s.chunk_tile[:, :], s.iota[:, bass.ds(i, 1)], -BIG, ALU.not_equal, ALU.mult))
                        turn.done(dve.tensor_tensor(line[:, :], line[:, :], s.top[:, :], ALU.add))
                        turn.done(dve.tensor_reduce(s.seg_max[:, bass.ds(i, 1)], line[:, :], AX_X, ALU.max))
                dve.wait_ge(s_sum, 1)
                for b in range(0, TILES, 8):
                    n = min(8, TILES - b)
                    dve.tensor_copy(s.agg[:, b:b + n, 0:used], acc[:, b:b + n, 0:used])

            @block.tensor
            def _(pe):
                if extra:
                    for h in range(2):
                        pe.sem_inc(s_side_read[h], 1)
                for b in range(0, 32, 8):
                    pe.matmul(acc[:, b:b + 8, :], s.zeros_b[:, 0:P], s.zeros_b[:, :], start=True, stop=False, skip_group_check=True)
                with pe.Fori(0, TURNS) as i:
                    tiles = load_tiles(s, pe, d.chunk_tile1, i)
                    for h in range(2):
                        if find_max:
                            pe.wait_ge(s_masked[h], i + 1)
                            pe.wait_ge(s_side_read[h], i + 1)
                            for u in range(U):
                                last = pe.transpose(side[h][:, u, :], masked[h][:, u, :], s.ident[:, :])
                            last.then_inc(s_side[h], 1)
                        if edge_max:
                            pe.wait_ge(s_side_read[h], i + 1)
                            for u in range(U):
                                last = pe.matmul(side[h][:, u, :], s.ident[:, :], s.max_rows[:, bass.ds(tiles[h * U + u] * P, P)],
                                                 start=True, stop=True)
                            last.then_inc(s_side[h], 1)
                        pe.wait_ge(ready[h], i * per + per)
                        pe.wait_ge(s_onehot[h], i + 1)
                        for u in range(U):
                            last = pe.matmul(acc[:, bass.ds(tiles[h * U + u], 1), 0:used], onehot[h][:, u, :],
                                             scaled[h][:, u, 0:used], start=False, stop=False, skip_group_check=True)
                        last.then_inc(s_added[h], 1)
                pe.drain().then_inc(s_sum, 1)


def load_tiles(s, pe, chunk_tile, i):
    pe.reg_load(s.tile_regs, row_of(chunk_tile[bass.ds(i * (2 * U), 2 * U)]))
    return [pe.snap(r, min_val=0, max_val=TILES - 1) for r in s.tile_regs]


def gated_pass(nc, s, d):
    with Phase(nc) as ctx:
        sb = lambda n, shape, dt=F32: ctx.enter_context(nc.sbuf_tensor(f"gated_{n}", shape, dt))
        sem = lambda n: ctx.semaphore(f"gated_{n}")
        two = lambda n, shape, dt=F32: [sb(f"{n}{h}", shape, dt) for h in range(2)]
        edges = two("edges", [P, U, META2])
        stage = two("stage", [P, U], I32)
        rows = two("rows", [P, U, WQ])
        onehot = two("onehot", [P, U, P])
        onehot_b = two("onehot_b", [P, U, P], BF16)
        turned = two("turned", [P, U, P])
        prod = two("prod", [P, U, GDIM])
        adapt = two("adapt", [P, U])
        coef = two("coef", [P, U])
        gate = two("gate", [P, U, F])
        msg = two("msg", [P, U, 64])
        acc = ctx.enter_context(nc.psum_tensor("gated_acc", [P, 32, 64], F32))
        turn_ps = [ctx.enter_context(nc.psum_tensor(f"gated_turn{h}", [P, U, P], BF16)) for h in range(2)]
        p_ps = [ctx.enter_context(nc.psum_tensor(f"gated_p{h}", [P, U, 64], F32)) for h in range(2)]
        pair = lambda n: [sem(f"{n}{h}") for h in range(2)]
        s_edges, s_staged, s_rows, s_onehot = pair("s_edges"), pair("s_staged"), pair("s_rows"), pair("s_onehot")
        s_turned, s_copied, s_p, s_msg, s_added = pair("s_turned"), pair("s_copied"), pair("s_p"), pair("s_msg"), pair("s_added")
        s_go = sem("s_go")
        s_step = sem("s_step")
        s_sum = sem("s_sum")
        v = d.sorted2.rearrange("(p k) w -> p k w", p=P)
        STEPS = 10
        with nc.Block() as block:
            @block.sync
            def _(sp):
                for h in range(2):
                    sp.sem_inc(s_added[h], 1)
                with sp.Fori(0, TURNS) as i:
                    for h in range(2):
                        sp.wait_ge(s_added[h], i + 1)
                        sp.dma_start(edges[h][:, :, :], v[:, bass.ds(i * (2 * U) + h * U, U), :]).then_inc(s_edges[h], 16)

            @block.scalar
            def _(act):
                with act.Fori(0, TURNS) as i:
                    for h in range(2):
                        act.wait_ge(s_edges[h], i * 16 + 16)
                        act.copy(stage[h][:, :], edges[h][:, :, F]).then_inc(s_staged[h], 1)
                        act.wait_ge(s_turned[h], i + 1)
                        act.copy(turned[h][:, :, :], turn_ps[h][:, :, :]).then_inc(s_copied[h], 1)

            @block.gpsimd
            def _(pool):
                with pool.Fori(0, TURNS) as i:
                    for h in range(2):
                        pool.wait_ge(s_staged[h], i + 1)
                        pool.sem_inc(s_go, 1)
                        for u in range(U):
                            pool.indirect_dma_start(rows[h][:, u, :], None, d.table2,
                                                    bass.IndirectOffsetOnAxis(ap=stage[h][:, u:u + 1], axis=0)).then_inc(s_rows[h], 16)

            @block.vector
            def _(dve):
                with dve.Fori(0, TURNS) as i:
                    turn = Steps(dve, s_step, i * STEPS)
                    for h in range(2):
                        r, e = rows[h], edges[h]
                        dve.wait_ge(s_edges[h], i * 16 + 16)
                        for u in range(U):
                            dve.tensor_scalar(onehot_b[h][:, u, :], s.iota[:, :], e[:, u, F + 1:F + 2], None, ALU.is_equal)
                            last = dve.tensor_scalar(onehot[h][:, u, :], s.iota[:, :], e[:, u, F + 1:F + 2], None, ALU.is_equal)
                        last.then_inc(s_onehot[h], 1)
                        dve.wait_ge(s_p[h], i + 1)
                        dve.wait_ge(s_rows[h], i * (16 * U) + 16 * U)
                        turn.done(dve.tensor_tensor(prod[h][:, :, :], p_ps[h][:, :, 0:GDIM], r[:, :, F:F + GDIM], ALU.mult))
                        dve.tensor_tensor(coef[h][:, :], e[:, :, F + 2], r[:, :, F + GDIM], ALU.mult)
                        turn.done(dve.tensor_reduce(adapt[h][:, :], prod[h][:, :, :], AX_X, ALU.add))
                        turn.done(dve.tensor_tensor(gate[h][:, :, :], e[:, :, 0:F], bc(adapt[h][:, :], F), ALU.add))
                        turn.done(dve.tensor_tensor(gate[h][:, :, :], gate[h][:, :, :], r[:, :, 0:F], ALU.mult))
                        dve.tensor_copy(msg[h][:, :, F], r[:, :, F + GDIM])
                        turn.done(dve.tensor_tensor(msg[h][:, :, 0:F], gate[h][:, :, :], bc(coef[h][:, :], F), ALU.mult))
                        dve.sem_inc(s_msg[h], 1)
                dve.wait_ge(s_sum, 1)
                for b in range(0, TILES, 8):
                    n = min(8, TILES - b)
                    dve.tensor_copy(s.agg[:, b:b + n, 0:F + 1], acc[:, b:b + n, 0:F + 1])

            @block.tensor
            def _(pe):
                for b in range(0, 32, 8):
                    pe.matmul(acc[:, b:b + 8, :], s.zeros_b[:, 0:P], s.zeros_b[:, :], start=True, stop=False, skip_group_check=True)
                with pe.Fori(0, TURNS) as i:
                    tiles = load_tiles(s, pe, d.chunk_tile2, i)
                    for h in range(2):
                        pe.wait_ge(s_onehot[h], i + 1)
                        for u in range(U):
                            last = pe.transpose(turn_ps[h][:, u, :], onehot_b[h][:, u, :], s.ident_b[:, :])
                        last.then_inc(s_turned[h], 1)
                        pe.wait_ge(s_copied[h], i + 1)
                        for u in range(U):
                            last = pe.matmul(p_ps[h][:, u, 0:GDIM], turned[h][:, u, :], s.pnode[:, bass.ds(tiles[h * U + u], 1), :],
                                             start=True, stop=True)
                        last.then_inc(s_p[h], 1)
                        pe.wait_ge(s_msg[h], i + 1)
                        for u in range(U):
                            last = pe.matmul(acc[:, bass.ds(tiles[h * U + u], 1), 0:F + 1], onehot[h][:, u, :],
                                             msg[h][:, u, 0:F + 1], start=False, stop=False, skip_group_check=True)
                        last.then_inc(s_added[h], 1)
                pe.drain().then_inc(s_sum, 1)


def sage_phase(nc, s, d, layer, w_self, w_neigh, bias):
    with Phase(nc) as ctx:
        sb = lambda n, shape, dt=F32: ctx.enter_context(nc.sbuf_tensor(f"{layer}_{n}", shape, dt))
        sem = lambda n: ctx.semaphore(f"{layer}_{n}")
        both = sb("both", [P, TILES, 2 * F])
        w = sb("w", [2 * F, F])
        b = sb("b", [P, F])
        deg = sb("deg", [P, TILES])
        res = sb("res", [P, TILES, F])
        tmp = sb("tmp", [P, TILES, F])
        part = sb("part", [P, NG, 2 * F])
        part_t = sb("part_t", [2 * F, NG, P])
        t_ps = ctx.enter_context(nc.psum_tensor(f"{layer}_t", [P, 8, P], F32))
        o_ps = ctx.enter_context(nc.psum_tensor(f"{layer}_o", [P, NG, 64], F32))
        s_w = sem("s_w")
        s_step = sem("s_step")
        s_both = sem("s_both")
        s_part = sem("s_part")
        s_t = sem("s_t")
        s_tc = sem("s_tc")
        s_o = sem("s_o")
        s_res = sem("s_res")
        s_var = sem("s_var")
        s_std = sem("s_std")
        s_h = sem("s_h")
        s_out = sem("s_out")
        s_back = sem("s_back")
        first = layer == "sage1"
        with nc.Block() as block:
            @block.sync
            def _(sp):
                sp.dma_start(w[0:F, :], w_self).then_inc(s_w, 16)
                sp.dma_start(w[F:2 * F, :], w_neigh).then_inc(s_w, 16)
                sp.dma_start(b[:, :], row_of(bias).broadcast_to([P, F])).then_inc(s_w, 16)
                if first:
                    sp.wait_ge(s_h, 1)
                    put_table(sp, d.table, s.tab[:, :, 0:W0], W0, s_out)
                    sp.wait_ge(s_out, 16)
                else:
                    sp.dma_start(d.seg_max.rearrange("(t p) -> p t", p=P), s.seg_max[:, 0:TILES]).then_inc(s_out, 16)
                    sp.wait_ge(s_out, 16)
                    sp.dma_start(s.max_rows[:, :], row_of(d.seg_max).broadcast_to([P, NODES])).then_inc(s_back, 16)
                    sp.wait_ge(s_back, 16)

            @block.scalar
            def _(act):
                act.wait_ge(s_both, 1)
                with act.Fori(0, NTURNS) as i:
                    act.copy(part[:, :, :], both[:, bass.ds(i * NG, NG), :]).then_inc(s_part, 1)
                    act.wait_ge(s_t, i + 1)
                    act.copy(part_t[:, :, :], t_ps[0:2 * F, 0:NG, :]).then_inc(s_tc, 1)
                    act.wait_ge(s_o, i + 1)
                    act.sem_inc(s_part, 1)
                if not first:
                    layernorm_relu(None, act, s, None, None, None, s.stat, None, s_var, s_std, 1)

            @block.tensor
            def _(pe):
                pe.wait_ge(s_w, 48)
                with pe.Fori(0, NTURNS) as i:
                    pe.wait_ge(s_part, i * 2 + 1)
                    for j in range(NG):
                        last = pe.transpose(t_ps[0:2 * F, j, :], part[:, j, :], s.ident[:, :])
                    last.then_inc(s_t, 1)
                    pe.wait_ge(s_tc, i + 1)
                    pe.wait_ge(s_res, i + 1)
                    for j in range(NG):
                        last = pe.matmul(o_ps[:, j, 0:F], part_t[:, j, :], w[:, :], start=True, stop=True)
                    last.then_inc(s_o, 1)

            @block.vector
            def _(dve):
                steps = Steps(dve, s_step)
                dve.sem_inc(s_res, 1)
                steps.done(dve.tensor_scalar(deg[:, :], s.agg[:, :, F], 1.0, None, ALU.max))
                steps.done(dve.reciprocal(deg[:, :], deg[:, :]))
                dve.tensor_copy(both[:, :, 0:F], s.h[:, :, :])
                dve.tensor_tensor(both[:, :, F:], s.agg[:, :, 0:F], bc(deg[:, :], F), ALU.mult).then_inc(s_both, 1)
                dve.wait_ge(s_w, 48)
                with dve.Fori(0, NTURNS) as i:
                    dve.wait_ge(s_o, i + 1)
                    dve.tensor_tensor(res[:, bass.ds(i * NG, NG), :], o_ps[:, :, 0:F], mid(b[:, :], NG), ALU.add).then_inc(s_res, 1)
                dve.wait_ge(s_res, NTURNS + 1)
                if first:
                    dve.tensor_scalar(s.h[:, :, :], res[:, :, :], 0.0, None, ALU.max)
                    dve.tensor_scalar(s.tab[:, :, 0:F], res[:, :, :], 0.0, None, ALU.max).then_inc(s_h, 1)
                else:
                    steps.done(dve.tensor_tensor(s.x[:, :, :], s.x[:, :, :], res[:, :, :], ALU.add))
                    layernorm_relu(dve, None, s, s.x[:, :, :], s.h[:, :, :], tmp[:, :, :], s.stat, steps, s_var, s_std, 1)


def relation_phase(nc, s, d):
    with Phase(nc) as ctx:
        sb = lambda n, shape, dt=F32: ctx.enter_context(nc.sbuf_tensor(f"rel_{n}", shape, dt))
        sem = lambda n: ctx.semaphore(f"rel_{n}")
        R2 = RELS // 2
        w1 = sb("w1", [F, RELS, F])
        w2 = sb("w2", [2 * F, R2, 2 * F])
        b1 = sb("b1", [2 * F, 1])
        part = sb("part", [P, NG, F])
        part_t = sb("part_t", [F, NG * P])
        hid = [sb(f"hid{m}", [2 * F, NG * P]) for m in range(R2)]
        out = [sb(f"out{m}", [P, RELS * F]) for m in range(NG)]
        t_ps = ctx.enter_context(nc.psum_tensor("rel_t", [P, 8, P], F32))
        z_ps = [ctx.enter_context(nc.psum_tensor(f"rel_z{m}", [P, 8 * P], F32)) for m in range(2)]
        o_ps = [ctx.enter_context(nc.psum_tensor(f"rel_o{m}", [P, 512], F32)) for m in range(2)]
        s_pe_go = sem("s_pe_go")
        s_blank, s_w, s_part, s_t, s_tc, s_z, s_hid, s_o, s_oc, s_out = (
            sem(n) for n in ("s_blank", "s_w", "s_part", "s_t", "s_tc", "s_z", "s_hid", "s_o", "s_oc", "s_out"))
        table = d.table_r.rearrange("(t p r) w -> t p (r w)", p=P, r=RELS)
        with nc.Block() as block:
            @block.sync
            def _(sp):
                sp.dma_start(w1[:, :, :], d.L1_gnn_weight1.rearrange("r i j -> i r j")).then_inc(s_w, 16)
                for k in range(2):
                    sp.dma_start(b1[k * F:(k + 1) * F, :], column(d.L1_gnn_bias1)).then_inc(s_w, 16)
                sp.wait_ge(s_blank, 1)
                for k in range(2):
                    sp.dma_start(w2[k * F:(k + 1) * F, :, k * F:(k + 1) * F],
                                 d.L1_gnn_weight2.rearrange("(m k) j o -> k j m o", k=2)[k]).then_inc(s_w, 16)
                sp.dma_start(out[0][:, 0:F], row_of(d.L1_gnn_bias1).broadcast_to([P, F])).then_inc(s_out, 16)
                with sp.Fori(0, NTURNS) as i:
                    for j in range(NG):
                        sp.wait_ge(s_oc, i * NG + (j + 2))
                        sp.dma_start(table[bass.ds(i * NG + j, 1), :, :].rearrange("a p w -> (a p) w"), out[j][:, :]).then_inc(s_out, 16)
                sp.wait_ge(s_out, 16 * TILES + 16)

            @block.scalar
            def _(act):
                act.sem_inc(s_hid, 1)
                act.sem_inc(s_hid, 1)
                act.wait_ge(s_w, 80)
                with act.Fori(0, NTURNS) as i:
                    act.wait_ge(s_t, i + 1)
                    act.copy(part[:, :, :], s.h[:, bass.ds(i * NG, NG), :]).then_inc(s_part, 1)
                    act.wait_ge(s_t, i + 2)
                    act.wait_ge(s_z, i * R2 + 1)
                    act.copy(part_t[:, :], t_ps[0:F, 0:NG, :].rearrange("p g n -> p (g n)")).then_inc(s_tc, 1)
                    act.wait_ge(s_o, i * NG + 1)
                    for m in range(R2):
                        act.wait_ge(s_z, i * R2 + (m + 2))
                        act.activation(hid[m][:, :], z_ps[m % 2][0:2 * F, 0:NG * P], ACT.Relu, bias=b1[:, 0:1]).then_inc(s_hid, 1)

            @block.tensor
            def _(pe):
                pe.sem_inc(s_t, 1)
                pe.sem_inc(s_z, 1)
                pe.sem_inc(s_o, 1)
                pe.wait_ge(s_w, 80)
                with pe.Fori(0, NTURNS) as i:
                    pe.wait_ge(s_part, i + 1)
                    pe.sem_inc(s_pe_go, 1)
                    for j in range(NG):
                        last = pe.transpose(t_ps[0:F, j, :], part[:, j, :], s.ident[:, :])
                    last.then_inc(s_t, 1)
                    pe.wait_ge(s_tc, i + 1)
                    for m in range(R2):
                        pe.wait_ge(s_hid, i * R2 + (m + 1))
                        pe.sem_inc(s_pe_go, 1)
                        for c, n in ((0, 512), (512, NG * P - 512)):
                            last = pe.matmul(z_ps[m % 2][0:2 * F, c:c + n], w1[:, 2 * m:2 * m + 2, :].rearrange("i r j -> i (r j)"),
                                             part_t[:, c:c + n], start=True, stop=True)
                        last.then_inc(s_z, 1)
                    pe.wait_ge(s_hid, i * R2 + (R2 + 2))
                    for j in range(NG):
                        pe.wait_ge(s_oc, i * NG + (j + 1))
                        for m in range(R2):
                            last = pe.matmul(o_ps[j % 2][:, m * 2 * F:(m + 1) * 2 * F], hid[m][:, j * P:(j + 1) * P], w2[:, m, :],
                                             start=True, stop=True)
                        last.then_inc(s_o, 1)

            @block.vector
            def _(dve):
                dve.memset(w2[:, :, :], 0.0).then_inc(s_blank, 1)
                dve.sem_inc(s_oc, 1)
                with dve.Fori(0, NTURNS) as i:
                    dve.wait_ge(s_out, i * (16 * NG) + 16)
                    for j in range(NG):
                        dve.wait_ge(s_o, i * NG + (j + 2))
                        dve.tensor_copy(out[j][:, :], o_ps[j % 2][:, 0:RELS * F]).then_inc(s_oc, 1)


def join_phase(nc, s, d, name, stage):
    with Phase(nc) as ctx:
        sb = lambda n, shape, dt=F32: ctx.enter_context(nc.sbuf_tensor(f"{name}_{n}", shape, dt))
        sem = lambda n: ctx.semaphore(f"{name}_{n}")
        rows = sb("rows", [P, 2, F])
        tmp = sb("tmp", [P, TILES, F])
        y = sb("y", [P, TILES, F])
        shift = sb("shift", [P, SLOTS]) if stage == "relation" else None
        den = sb("den", [P, TILES])
        s_w, s_step, s_var, s_std, s_h, s_out, s_arg, s_exp = (
            sem(n) for n in ("s_w", "s_step", "s_var", "s_std", "s_h", "s_out", "s_arg", "s_exp"))
        vectors = {"relation": [d.L1_gnn_bias2], "gated": [d.L2_gnn_gamma, d.L2_gnn_beta], "softmax": []}[stage]
        with nc.Block() as block:
            @block.sync
            def _(sp):
                for n, vec in enumerate(vectors):
                    sp.dma_start(rows[:, n, :], row_of(vec).broadcast_to([P, F])).then_inc(s_w, 16)
                sp.wait_ge(s_h, 1)
                if stage == "relation":
                    put_table(sp, d.table2, s.tab[:, :, :], WQ, s_out)
                    sp.wait_ge(s_out, 16)
                elif stage == "gated":
                    put_table(sp, d.table, s.tab[:, :, 0:W0], W0, s_out)
                    sp.wait_ge(s_out, 16)
                else:
                    sp.dma_start(node_rows(d.out, 0, P, 0, TILES - 1), y[:, 0:TILES - 1, :]).then_inc(s_out, 16)
                    sp.dma_start(d.out[(TILES - 1) * P:N, :], y[0:LAST, TILES - 1, :]).then_inc(s_out, 16)
                    sp.wait_ge(s_out, 32)

            @block.scalar
            def _(act):
                if stage == "relation":
                    act.wait_ge(s_arg, 1)
                    act.activation(s.ex[:, :], shift[:, :], ACT.Exp).then_inc(s_exp, 1)
                if stage == "softmax":
                    act.wait_ge(s_arg, 1)
                    act.activation(tmp[:, :, :], tmp[:, :, :], ACT.Exp).then_inc(s_exp, 1)
                    return
                layernorm_relu(None, act, s, None, None, None, s.stat, None, s_var, s_std, 1)
                if stage == "gated":
                    layernorm_relu(None, act, s, None, None, None, s.stat, None, s_var, s_std, 2)

            @block.vector
            def _(dve):
                steps = Steps(dve, s_step)
                agg = s.agg[:, :, 0:F]
                if stage == "relation":
                    steps.done(dve.tensor_tensor(shift[:, :], s.weight1[:, :], s.edge_top[:, :], ALU.subtract))
                    dve.tensor_scalar(shift[:, :], shift[:, :], 0.0, None, ALU.min).then_inc(s_arg, 1)
                    dve.wait_ge(s_w, 16)
                    steps.done(dve.tensor_tensor(y[:, :, :], agg, mid(rows[:, 0, :], TILES), ALU.add))
                    steps.done(dve.scalar_tensor_tensor(s.x[:, :, :], y[:, :, :], 0.0, s.x[:, :, :], ALU.max, ALU.add))
                    layernorm_relu(dve, None, s, s.x[:, :, :], s.h[:, :, :], tmp[:, :, :], s.stat, steps, s_var, s_std, 1)
                    dve.tensor_copy(s.tab[:, :, F:F + GDIM], s.qnode[:, :, :])
                    dve.tensor_copy(s.tab[:, :, F + GDIM], s.nvec[:, :])
                    dve.tensor_copy(s.tab[:, :, 0:F], s.h[:, :, :]).then_inc(s_h, 1)
                    dve.wait_ge(s_exp, 1)
                elif stage == "gated":
                    steps.done(dve.tensor_scalar(den[:, :], s.agg[:, :, F], 1e-8, None, ALU.max))
                    steps.done(dve.reciprocal(den[:, :], den[:, :]))
                    steps.done(dve.tensor_tensor(tmp[:, :, :], agg, bc(den[:, :], F), ALU.mult))
                    steps.done(dve.tensor_tensor(s.h[:, :, :], s.h[:, :, :], tmp[:, :, :], ALU.add))
                    layernorm_relu(dve, None, s, s.h[:, :, :], y[:, :, :], tmp[:, :, :], s.stat, steps, s_var, s_std, 1, relu=False)
                    dve.wait_ge(s_w, 32)
                    steps.done(dve.tensor_tensor(y[:, :, :], y[:, :, :], mid(rows[:, 0, :], TILES), ALU.mult))
                    steps.done(dve.tensor_tensor(y[:, :, :], y[:, :, :], mid(rows[:, 1, :], TILES), ALU.add))
                    steps.done(dve.tensor_tensor(s.x[:, :, :], s.x[:, :, :], y[:, :, :], ALU.add))
                    layernorm_relu(dve, None, s, s.x[:, :, :], s.h[:, :, :], tmp[:, :, :], s.stat, steps, s_var, s_std, 2)
                    steps.done(dve.memset(s.tab[:, :, F:F + 1], 1.0))
                    dve.tensor_copy(s.tab[:, :, 0:F], s.h[:, :, :]).then_inc(s_h, 1)
                else:
                    steps.done(dve.tensor_scalar(den[:, :], s.agg[:, :, F], 1.0, None, ALU.max))
                    steps.done(dve.reciprocal(den[:, :], den[:, :]))
                    steps.done(dve.tensor_tensor(y[:, :, :], agg, bc(den[:, :], F), ALU.mult))
                    dve.tensor_scalar(tmp[:, :, :], y[:, :, :], 0.0, None, ALU.min).then_inc(s_arg, 1)
                    steps.done(dve.tensor_scalar(y[:, :, :], y[:, :, :], 0.0, None, ALU.max))
                    steps.done(dve.tensor_tensor(s.x[:, :, :], s.x[:, :, :], y[:, :, :], ALU.add))
                    dve.wait_ge(s_exp, 1)
                    steps.done(dve.tensor_scalar(tmp[:, :, :], tmp[:, :, :], 1.0, None, ALU.subtract))
                    dve.tensor_tensor(y[:, :, :], s.x[:, :, :], tmp[:, :, :], ALU.add).then_inc(s_h, 1)


def build(nc, x, src, dst, edge_attr_40, edge_type_8, edge_weight, edge_weight1, node_type_119, node_vec, out,
          L0_gnn_W_self1, L0_gnn_W_neigh1, L0_gnn_b1, L0_gnn_W_self2, L0_gnn_W_neigh2, L0_gnn_b2,
          L1_gnn_weight1, L1_gnn_weight2, L1_gnn_bias1, L1_gnn_bias2,
          L2_gnn_W1, L2_gnn_b1, L2_gnn_W2, L2_gnn_b2, L2_gnn_emb, L2_gnn_adaptW, L2_gnn_gamma, L2_gnn_beta):
    s, d = Store(), Store()
    d.x = x
    d.src = src
    d.dst = dst
    d.edge_attr_40 = edge_attr_40
    d.edge_type_8 = edge_type_8
    d.edge_weight = edge_weight
    d.edge_weight1 = edge_weight1
    d.node_type_119 = node_type_119
    d.node_vec = node_vec
    d.L0_gnn_W_self1 = L0_gnn_W_self1
    d.L0_gnn_W_neigh1 = L0_gnn_W_neigh1
    d.L0_gnn_b1 = L0_gnn_b1
    d.L0_gnn_W_self2 = L0_gnn_W_self2
    d.L0_gnn_W_neigh2 = L0_gnn_W_neigh2
    d.L0_gnn_b2 = L0_gnn_b2
    d.L1_gnn_weight1 = L1_gnn_weight1
    d.L1_gnn_weight2 = L1_gnn_weight2
    d.L1_gnn_bias1 = L1_gnn_bias1
    d.L1_gnn_bias2 = L1_gnn_bias2
    d.L2_gnn_W1 = L2_gnn_W1
    d.L2_gnn_b1 = L2_gnn_b1
    d.L2_gnn_W2 = L2_gnn_W2
    d.L2_gnn_b2 = L2_gnn_b2
    d.L2_gnn_emb = L2_gnn_emb
    d.L2_gnn_adaptW = L2_gnn_adaptW
    d.L2_gnn_gamma = L2_gnn_gamma
    d.L2_gnn_beta = L2_gnn_beta
    d.out = out
    with ExitStack() as ctx:
        ctx.enter_context(nc.allow_non_contiguous_dma(reason="one word per node or chunk"))
        sb = lambda n, shape, dt=F32: ctx.enter_context(nc.sbuf_tensor(n, shape, dt))
        dram = lambda n, shape, dt=F32: nc.dram_tensor(n, shape, dt).ap()
        d.table = dram("table", (NODES, W0))
        d.table2 = dram("table2", (NODES, WQ))
        d.table_r = dram("table_r", (NODES * RELS, F))
        d.sorted1 = dram("sorted1", (P * ROW, META1))
        d.sorted2 = dram("sorted2", (P * ROW, META2))
        d.chunk_tile1 = dram("chunk_tile1", (SLOT_COLS * P,), I32)
        d.chunk_tile2 = dram("chunk_tile2", (SLOT_COLS * P,), I32)
        d.seg_max = dram("seg_max_rows", (NODES,))
        d.zeros = dram("zeros_rows", (P * U * ATTR,))
        s.x = sb("x", [P, TILES, F])
        s.h = sb("h", [P, TILES, F])
        s.agg = sb("agg", [P, TILES, F + 1])
        s.tab = sb("tab", [P, TILES, WQ])
        s.stat = sb("stat", [P, 4, TILES])
        s.nvec = sb("nvec", [P, TILES])
        s.pnode = sb("pnode", [P, TILES, GDIM])
        s.qnode = sb("qnode", [P, TILES, GDIM])
        s.iota = sb("iota", [P, P])
        s.ident = sb("ident", [P, P])
        s.ident_b = sb("ident_b", [P, P], BF16)
        s.ones = sb("ones", [P, P])
        s.lower = sb("lower", [P, P])
        s.zeros = sb("zeros", [P, 512])
        s.zeros_b = sb("zeros_b", [P, 512], BF16)
        s.lane = sb("lane", [P, 1])
        s.eps = sb("eps", [P, 1])
        s.half_pi = sb("half_pi", [P, 1])
        s.iota_slot = sb("iota_slot", [P, SLOT_COLS])
        s.chunk_tile_i = sb("chunk_tile_i", [P, SLOTS], I32)
        s.chunk_tile = sb("chunk_tile", [P, SLOTS])
        s.tile_regs = [nc.tensor.alloc_register(f"tile{n}") for n in range(2 * U)]
        with ExitStack() as sorting:
            ss = lambda n, shape, dt=F32: sorting.enter_context(nc.sbuf_tensor(n, shape, dt))
            s.sentinel1 = ss("sentinel1", [P, SLOTS, META1])
            s.sentinel2 = ss("sentinel2", [P, 2 * U, META2])
            s.meta1 = ss("meta1", [P, CHUNKS, META1])
            s.meta2 = ss("meta2", [P, CHUNKS, META2 - F])
            s.cell = ss("cell", [P, CHUNKS], I32)
            s.tile_d = ss("tile_d", [P, CHUNKS])
            s.tile_s = ss("tile_s", [P, CHUNKS])
            s.rows1 = ss("rows1", [P, CHUNKS], I32)
            s.rows2 = ss("rows2", [P, CHUNKS], I32)
            setup_phase(nc, s, d)
            fill_phase(nc, s, d)
            rank_phase(nc, s, s.tile_d[:, :], s.rows1, s.chunk_tile_i[:, :], d.chunk_tile1, "rank1")
            rank_phase(nc, s, s.tile_s[:, :], s.rows2, None, d.chunk_tile2, "rank2")
            sort_phase(nc, s, d)
        s.edge1 = sb("edge1", [P, SLOTS, META1])
        s.lane1 = sb("lane1", [P, SLOTS])
        s.weight1 = sb("weight1", [P, SLOTS])
        s.top = sb("top", [P, SLOTS])
        s.edge_top = sb("edge_top", [P, SLOTS])
        s.ex = sb("ex", [P, SLOTS])
        s.seg_max = sb("seg_max", [P, TURNS])
        s.max_rows = sb("max_rows", [P, NODES])
        reload_phase(nc, s, d)
        source, related = s.edge1[:, :, 0], s.edge1[:, :, 1]
        edge_pass(nc, s, d, "sum1", d.table, W0, F + 1, source, find_max=True)
        sage_phase(nc, s, d, "sage1", d.L0_gnn_W_self1, d.L0_gnn_W_neigh1, d.L0_gnn_b1)
        edge_pass(nc, s, d, "sum2", d.table, W0, F + 1, source, join_max=True)
        sage_phase(nc, s, d, "sage2", d.L0_gnn_W_self2, d.L0_gnn_W_neigh2, d.L0_gnn_b2)
        relation_phase(nc, s, d)
        edge_pass(nc, s, d, "sum3", d.table_r, F, F, related, weight=s.weight1, edge_max=True)
        join_phase(nc, s, d, "join1", "relation")
        gated_pass(nc, s, d)
        join_phase(nc, s, d, "join2", "gated")
        edge_pass(nc, s, d, "sum4", d.table, W0, F + 1, source, weight=s.ex)
        join_phase(nc, s, d, "join3", "softmax")


_INS = ['x', 'src', 'dst', 'edge_attr_40', 'edge_type_8', 'edge_weight', 'edge_weight1', 'node_type_119', 'node_vec',
        'L0_gnn_W_self1', 'L0_gnn_W_neigh1', 'L0_gnn_b1', 'L0_gnn_W_self2', 'L0_gnn_W_neigh2', 'L0_gnn_b2',
        'L1_gnn_weight1', 'L1_gnn_weight2', 'L1_gnn_bias1', 'L1_gnn_bias2',
        'L2_gnn_W1', 'L2_gnn_b1', 'L2_gnn_W2', 'L2_gnn_b2', 'L2_gnn_emb', 'L2_gnn_adaptW', 'L2_gnn_gamma', 'L2_gnn_beta']


def kernel(**inputs):
    import numpy as _np
    import concourse.bacc as _bacc
    from concourse import mybir as _mybir
    from concourse.bass_utils import run_bass_kernel_spmd as _run

    nc = _bacc.Bacc("TRN2", target_bir_lowering=False, num_devices=1)
    arrays, args = {}, {}
    for name in _INS:
        a = _np.ascontiguousarray(inputs[name])
        arrays[f"in_{name}_dram"] = a
        args[name] = nc.dram_tensor(f"in_{name}_dram", a.shape, _mybir.dt.from_np(a.dtype), kind="ExternalInput").ap()
    args["out"] = nc.dram_tensor("out_dram", (N, F), F32, kind="ExternalOutput").ap()
    build(nc, **args)
    r = _run(nc, [arrays], core_ids=[0])
    return r.results[0]["out_dram"]
```

```python
from contextlib import ExitStack

import concourse.bass as bass
from concourse import mybir

P = 128
ALU = mybir.AluOpType
ACT = mybir.ActivationFunctionType
AX_X = mybir.AxisListType.X
F32 = mybir.dt.float32
BF16 = mybir.dt.bfloat16
I32 = mybir.dt.int32

N = 3125
E = 103125
F = 48
ATTR = 40
RELS = 8
GDIM = 32
KINDS = 119

TILES = -(-N // P)
LAST = N - (TILES - 1) * P
NODES = TILES * P
H = 4
G = 4
U = 8
GROUP = P * U
PAIRS = -(-E // (2 * GROUP))
GROUPS = 2 * PAIRS
CHUNKS = GROUPS * U
FULL = E // GROUP
TAIL = E - FULL * GROUP
TAIL_P, TAIL_U = divmod(TAIL, U)
BUCKETS = TILES + 1
TURNS = -(-(-(-E // P) + TILES) // 16)
SLOTS = TURNS * 16
PAD_CHUNKS = -(-(CHUNKS * P - E) // P)
ROW1 = SLOTS + PAD_CHUNKS
ROW2 = SLOTS + -(-(SLOTS * P - E) // P)
SLOT_COLS = -(-SLOTS // (P * G))
FREE_FROM = -(-E // P)
SRC, REL, LANE_D, WEIGHT, CUT, TILE_S, LANE_S = range(7)
META = 8
EDGE = F + META
MSG = 52
W0 = 96
BUCKET_COLS = 64
CUTOFF = 6.0
EPS = 1e-5
BIG = 1e38
NG = 5
NTURNS = TILES // NG
HALF_PI = 1.5707963267948966
assert FULL == GROUPS - 2 and N % P and TILES % NG == 0 and E // P + TILES <= SLOTS and H * G == 16 and BUCKETS <= TURNS and TURNS % H == 0


class Steps:

    def __init__(self, eng, sem, start=0):
        self.eng, self.sem, self.start, self.n = eng, sem, start, 0

    def done(self, ins):
        self.n += 1
        ins.then_inc(self.sem, 1)
        self.eng.wait_ge(self.sem, self.start + self.n)


class Phase(ExitStack):

    def __init__(self, nc):
        super().__init__()
        self.nc, self.sems = nc, []

    def semaphore(self, name):
        self.sems.append(self.nc.alloc_semaphore(name))
        return self.sems[-1]

    def __exit__(self, *error):
        self.nc.clear_and_free_semaphores(self.sems)
        self.nc.all_engine_barrier()
        return super().__exit__(*error)


def bc(ap, n):
    return ap.unsqueeze(len(ap.shape)).broadcast_to(list(ap.shape) + [n])


def mid(ap, n):
    return ap.unsqueeze(1).broadcast_to([ap.shape[0], n, ap.shape[1]])


def column(vector):
    return vector.rearrange("(p a) -> p a", a=1)


def row_of(vector):
    return vector.rearrange("(a f) -> a f", a=1)


def node_rows(dram, p0, p1, t0, t1):
    return dram[t0 * P:t1 * P, :].rearrange("(t p) f -> p t f", p=P)[p0:p1]


def put_table(eng, table, tile, words, sem):
    eng.dma_start(table.rearrange("(t p) w -> p t w", p=P)[:, :, 0:words], tile).then_inc(sem, 16)


def layernorm_relu(dve, act, s, x, h, tmp, stat, steps, ln_var, ln_std, turn, relu=True):
    if act is not None:
        act.wait_ge(ln_var, turn)
        act.activation(stat[:, 2, :], stat[:, 1, :], ACT.Sqrt, bias=s.eps[:, :], scale=1.0 / F).then_inc(ln_std, 1)
        return
    steps.done(dve.tensor_reduce(stat[:, 0, :], x, AX_X, ALU.add))
    steps.done(dve.tensor_scalar(stat[:, 0, :], stat[:, 0, :], 1.0 / F, None, ALU.mult))
    steps.done(dve.tensor_tensor(h, x, bc(stat[:, 0, :], F), ALU.subtract))
    steps.done(dve.tensor_tensor(tmp, h, h, ALU.mult))
    dve.tensor_reduce(stat[:, 1, :], tmp, AX_X, ALU.add).then_inc(ln_var, 1)
    dve.wait_ge(ln_std, turn)
    steps.done(dve.reciprocal(stat[:, 3, :], stat[:, 2, :]))
    steps.done(dve.tensor_tensor(h, h, bc(stat[:, 3, :], F), ALU.mult))
    if relu:
        steps.done(dve.tensor_scalar(h, h, 0.0, None, ALU.max))


class Store:
    pass


def setup_phase(nc, s, d):
    with Phase(nc) as ctx:
        sb = lambda n, shape, dt=F32: ctx.enter_context(nc.sbuf_tensor(n, shape, dt))
        sem = lambda n: ctx.semaphore(n)
        src_i = sb("src_i", [P, GROUPS, U], I32)
        dst_i = sb("dst_i", [P, GROUPS, U], I32)
        typ_i = sb("typ_i", [P, GROUPS, U], I32)
        dist = sb("dist", [P, GROUPS, U])
        w1 = sb("w1", [P, GROUPS, U])
        f_a = sb("f_a", [P, CHUNKS])
        f_b = sb("f_b", [P, CHUNKS])
        iota_i = sb("iota_i", [P, P], I32)
        lane_i = sb("lane_i", [P, 1], I32)
        iota_slot_i = sb("iota_slot_i", [P, SLOT_COLS, G], I32)
        cell = sb("cell", [P, CHUNKS], I32)
        tmp = sb("tmp", [P, TILES, F])
        emb_t = sb("emb_t", [GDIM, KINDS])
        emb = sb("emb", [KINDS, GDIM])
        adapt_t = sb("adapt_t", [GDIM, GDIM])
        adapt = sb("adapt", [GDIM, GDIM])
        emb_pq = sb("emb_pq", [KINDS, 2 * GDIM])
        kind_row = sb("kind_row", [P, NODES], I32)
        kind_f = sb("kind_f", [P, NODES])
        tr_ps = ctx.enter_context(nc.psum_tensor("tr_ps", [P, 512], F32))
        q_ps = ctx.enter_context(nc.psum_tensor("q_ps", [P, 512], F32))
        pq_ps = ctx.enter_context(nc.psum_tensor("pq_ps", [P, 4, 8, 64], F32))
        s_blank = sem("s_blank")
        s_edges = sem("s_edges")
        s_x = sem("s_x")
        s_small = sem("s_small")
        s_iota = sem("s_iota")
        s_const = sem("s_const")
        s_kind = sem("s_kind")
        s_kindf = sem("s_kindf")
        s_cos_in = sem("s_cos_in")
        s_cos = sem("s_cos")
        s_dve = sem("s_dve")
        s_var = sem("s_var")
        s_std = sem("s_std")
        s_tr = sem("s_tr")
        s_trc = sem("s_trc")
        s_q = sem("s_q")
        s_qc = sem("s_qc")
        s_pq = sem("s_pq")
        s_h = sem("s_h")
        s_out = sem("s_out")
        flat = lambda t: t[:, :, :].rearrange("p g u -> p (g u)")
        with nc.Block() as block:
            @block.sync
            def _(sp):
                sp.wait_ge(s_blank, 1)
                sp.dma_start(s.x[:, 0:TILES - 1, :], node_rows(d.x, 0, P, 0, TILES - 1)).then_inc(s_x, 16)
                sp.dma_start(s.x[0:LAST, TILES - 1, :], d.x[(TILES - 1) * P:N, :]).then_inc(s_x, 16)
                for dram, tile in ((d.dst, dst_i), (d.src, src_i), (d.edge_type_8, typ_i), (d.edge_weight, dist), (d.edge_weight1, w1)):
                    v = dram if len(dram.shape) == 1 else dram.rearrange("e a -> (e a)")
                    cut = FULL * GROUP + TAIL_P * U
                    sp.dma_start(tile[:, 0:FULL, :], v[0:FULL * GROUP].rearrange("(g p u) -> p g u", p=P, u=U)).then_inc(s_edges, 16)
                    sp.dma_start(tile[0:TAIL_P, FULL, :], v[FULL * GROUP:cut].rearrange("(p u) -> p u", u=U)).then_inc(s_edges, 16)
                    sp.dma_start(tile[TAIL_P:TAIL_P + 1, FULL, 0:TAIL_U], row_of(v[cut:E])).then_inc(s_edges, 16)
                sp.wait_ge(s_h, 2)
                put_table(sp, d.table, s.tab[:, :, 0:W0], W0, s_out)
                sp.wait_ge(s_out, 16)

            @block.scalar
            def _(act):
                act.dma_start(emb[:, :], d.L2_gnn_emb).then_inc(s_small, 16)
                act.dma_start(adapt[:, :], d.L2_gnn_adaptW).then_inc(s_small, 16)
                act.dma_start(kind_row[:, 0:N], row_of(d.node_type_119).broadcast_to([P, N])).then_inc(s_kind, 16)
                act.wait_ge(s_blank, 1)
                act.dma_start(s.nvec[:, 0:TILES - 1], d.node_vec[0:(TILES - 1) * P].rearrange("(t p) -> p t", p=P)).then_inc(s_small, 16)
                act.dma_start(s.nvec[0:LAST, TILES - 1:TILES], column(d.node_vec[(TILES - 1) * P:N])).then_inc(s_small, 16)
                layernorm_relu(None, act, s, None, None, None, s.stat, None, s_var, s_std, 1)
                act.wait_ge(s_cos_in, 1)
                act.activation(f_b[:, :], f_a[:, :], ACT.Sin, bias=s.half_pi[:, :], scale=-2.0 * HALF_PI / CUTOFF).then_inc(s_cos, 1)

            @block.gpsimd
            def _(pool):
                pool.iota(iota_i[:, :], [[1, P]], base=0, channel_multiplier=0).then_inc(s_iota, 1)
                pool.iota(lane_i[:, :], [[1, 1]], base=0, channel_multiplier=1).then_inc(s_iota, 1)
                pool.iota(iota_slot_i[:, :, :], [[P * G, SLOT_COLS], [1, G]], base=0, channel_multiplier=G).then_inc(s_iota, 1)

            @block.tensor
            def _(pe):
                pe.wait_ge(s_const, 1)
                pe.wait_ge(s_small, 64)
                pe.transpose(tr_ps[0:GDIM, 0:KINDS], emb[:, :], s.ident[0:KINDS, 0:KINDS])
                pe.transpose(tr_ps[0:GDIM, P:P + GDIM], adapt[:, :], s.ident[0:GDIM, 0:GDIM]).then_inc(s_tr, 1)
                pe.wait_ge(s_trc, 2)
                pe.matmul(q_ps[0:KINDS, 0:GDIM], emb_t[:, :], adapt_t[:, :], start=True, stop=True).then_inc(s_q, 1)
                pe.wait_ge(s_kindf, 1)
                pe.wait_ge(s_qc, 2)
                for t in range(TILES):
                    last = pe.matmul(pq_ps[:, t // 8, t % 8, :], kind_f[0:KINDS, t * P:(t + 1) * P], emb_pq[:, :],
                                     start=True, stop=True)
                last.then_inc(s_pq, 1)

            @block.vector
            def _(dve):
                dve.memset(s.x[:, :, :], 0.0)
                dve.memset(s.nvec[:, :], 0.0)
                for tile, value in ((dst_i, NODES), (src_i, NODES), (typ_i, 0), (dist, 0.0), (w1, 0.0)):
                    last = dve.memset(tile[:, FULL:GROUPS, :], value)
                last.then_inc(s_blank, 1)
                dve.memset(s.tab[:, :, :], 1.0)
                dve.memset(s.eps[:, :], EPS)
                dve.memset(s.half_pi[:, :], HALF_PI)
                dve.memset(s.ones[:, :], 1.0)
                dve.memset(s.zeros[:, :], 0.0)
                dve.memset(s.zeros_b[:, :], 0.0)
                dve.memset(s.sentinel1[:, :, :], 0.0)
                last = dve.memset(s.sentinel2[:, :, :], 0.0)
                steps = Steps(dve, s_dve)
                steps.done(last)
                dve.memset(s.sentinel1[:, :, F + LANE_D:F + LANE_D + 1], -1.0)
                dve.memset(s.sentinel1[:, :, F + LANE_S:F + LANE_S + 1], -1.0)
                dve.memset(s.sentinel1[:, :, F + TILE_S:F + TILE_S + 1], float(TILES))
                steps.done(dve.memset(s.sentinel2[:, :, F + 1:F + 2], -1.0))
                dve.wait_ge(s_iota, 3)
                dve.tensor_copy(s.lane[:, :], lane_i[:, :])
                for row in (ROW1, ROW2):
                    dve.tensor_scalar(s.lane_row[row], lane_i[:, :], row, None, ALU.mult)
                dve.tensor_copy(s.iota_slot[:, :, :], iota_slot_i[:, :, :])
                dve.tensor_copy(s.iota_b[:, :], iota_i[:, :])
                steps.done(dve.tensor_copy(s.iota[:, :], iota_i[:, :]))
                dve.tensor_scalar(s.lower[:, :], s.iota[:, :], s.lane[:, 0:1], None, ALU.is_gt)
                dve.tensor_scalar(s.ident_b[:, :], s.iota[:, :], s.lane[:, 0:1], None, ALU.is_equal)
                dve.tensor_scalar(s.ident[:, :], s.iota[:, :], s.lane[:, 0:1], None, ALU.is_equal).then_inc(s_const, 1)

                dve.wait_ge(s_x, 32)
                layernorm_relu(dve, None, s, s.x[:, :, :], s.h[:, :, :], tmp[:, :, :], s.stat, steps, s_var, s_std, 1)
                dve.tensor_copy(s.tab[:, :, 0:F], s.h[:, :, :]).then_inc(s_h, 1)

                dve.wait_ge(s_tr, 1)
                dve.tensor_copy(emb_t[:, :], tr_ps[0:GDIM, 0:KINDS]).then_inc(s_trc, 1)
                dve.tensor_copy(adapt_t[:, :], tr_ps[0:GDIM, P:P + GDIM]).then_inc(s_trc, 1)
                dve.tensor_copy(emb_pq[:, 0:GDIM], emb[:, :]).then_inc(s_qc, 1)
                dve.wait_ge(s_q, 1)
                dve.tensor_copy(emb_pq[:, GDIM:], q_ps[0:KINDS, 0:GDIM]).then_inc(s_qc, 1)
                dve.wait_ge(s_kind, 16)
                steps.done(dve.memset(kind_row[:, N:NODES], 0))
                dve.tensor_scalar(kind_f[:, :], kind_row[:, :], s.lane[:, 0:1], None, ALU.is_equal).then_inc(s_kindf, 1)
                dve.wait_ge(s_pq, 1)
                for b in range(0, TILES, 8):
                    n = min(8, TILES - b)
                    dve.tensor_copy(s.tab[:, b:b + n, F + 1:F + 1 + GDIM], pq_ps[:, b // 8, 0:n, 0:GDIM])
                    last = dve.tensor_copy(s.qnode[:, b:b + n, 0:GDIM], pq_ps[:, b // 8, 0:n, GDIM:])
                last.then_inc(s_h, 1)
                dve.tensor_copy(s.qnode[:, :, GDIM], s.nvec[:, :])

                dve.wait_ge(s_edges, 15 * 16)
                field = lambda n: s.meta[:, :, n]
                dve.tensor_scalar(cell[:, :], flat(dst_i), 7, None, ALU.logical_shift_right)
                dve.tensor_copy(f_b[:, :], flat(dst_i))
                steps.done(dve.tensor_copy(field(SRC), flat(src_i)))
                dve.tensor_copy(field(WEIGHT), flat(w1))
                dve.memset(field(META - 1), 0.0)
                steps.done(dve.tensor_copy(s.tile_d[:, :], cell[:, :]))
                dve.tensor_scalar(cell[:, :], flat(src_i), 7, None, ALU.logical_shift_right)
                steps.done(dve.tensor_copy(f_a[:, :], flat(typ_i)))
                dve.scalar_tensor_tensor(field(REL), field(SRC), float(RELS), f_a[:, :], ALU.mult, ALU.add)
                dve.scalar_tensor_tensor(field(LANE_D), s.tile_d[:, :], -float(P), f_b[:, :], ALU.mult, ALU.add)
                steps.done(dve.tensor_copy(field(TILE_S), cell[:, :]))
                dve.scalar_tensor_tensor(field(LANE_S), field(TILE_S), -float(P), field(SRC), ALU.mult, ALU.add)
                steps.done(dve.tensor_scalar(f_b[:, :], flat(dist), -1.0, None, ALU.mult))
                steps.done(dve.tensor_tensor(f_b[:, :], f_b[:, :], flat(dist), ALU.max))
                dve.tensor_scalar(f_a[:, :], f_b[:, :], CUTOFF, None, ALU.min).then_inc(s_cos_in, 1)
                dve.wait_ge(s_cos, 1)
                steps.done(dve.tensor_scalar(f_b[:, :], f_b[:, :], 0.5, 0.5, ALU.mult, ALU.add))
                dve.scalar_tensor_tensor(field(CUT), flat(dist), CUTOFF, f_b[:, :], ALU.is_lt, ALU.mult)


class Ranks:

    def __init__(self, sb, ps, width, row):
        self.width, self.row = width, row
        self.match = sb("rank_match", [P, width], BF16)
        self.cum = sb("rank_cum", [P, width])
        self.term = sb("rank_term", [P, width])
        self.pos = sb("rank_pos", [P, width])
        self.none = sb("rank_none", [P, width])
        self.cell = sb("rank_cell", [P, width], I32)
        self.rows = sb("rank_rows", [P, width], I32)
        self.count = sb("rank_count", [P, BUCKET_COLS])
        self.base = sb("rank_base", [P, BUCKET_COLS])
        self.first = sb("rank_first", [P, BUCKET_COLS])
        self.small = sb("rank_small", [P, BUCKET_COLS])
        self.small_i = sb("rank_small_i", [P, BUCKET_COLS], I32)
        self.blank = sb("rank_blank", [P, BUCKET_COLS])
        self.cmp = sb("rank_cmp", [P, SLOT_COLS, G, BUCKET_COLS])
        self.tile_f = sb("rank_tile_f", [P, SLOT_COLS, G])
        self.tile_i = sb("rank_tile_i", [P, SLOT_COLS, G], I32)
        self.tail = sb("rank_tail", [P, BUCKET_COLS])
        self.tail_i = sb("rank_tail_i", [P, BUCKET_COLS], I32)
        self.ps = ps

    def clear(self, dve, steps):
        dve.memset(self.pos[:, :], 0.0)
        dve.memset(self.none[:, :], 0.0)
        dve.memset(self.count[:, :], 0.0)
        steps.done(dve.memset(self.blank[:, :], 0.0))

    def count_bucket(self, dve, s, key, t, steps):
        steps.done(dve.tensor_scalar(self.match[:, :], key, s.iota[:, bass.ds(t, 1)], None, ALU.is_equal))
        steps.done(dve.tensor_reduce(self.count[:, bass.ds(t, 1)], self.match[:, :], AX_X, ALU.add))

    def sums(self, pe, s, done):
        pe.matmul(self.ps[:, 0, :], s.ones[:, :], self.count[:, :], start=True, stop=True)
        pe.matmul(self.ps[:, 1, :], s.lower[:, :], self.count[:, :], start=True, stop=True).then_inc(done, 1)

    def bases(self, dve, s, steps, tiles_ready):
        small, small_i, first, base = self.small, self.small_i, self.first, self.base
        steps.done(dve.tensor_scalar(small[:, :], self.ps[:, 0, :], float(P - 1), None, ALU.add))
        steps.done(dve.tensor_copy(small_i[:, :], small[:, :]))
        steps.done(dve.tensor_scalar(small_i[:, :], small_i[:, :], 7, None, ALU.logical_shift_right))
        steps.done(dve.tensor_copy(small[:, :], small_i[:, :]))
        steps.done(dve.tensor_tensor_scan(first[:, :], small[:, :], self.blank[:, :], 0.0, ALU.add, ALU.add))
        steps.done(dve.tensor_tensor(first[:, :], first[:, :], small[:, :], ALU.subtract))
        steps.done(dve.memset(first[:, TILES:BUCKETS], float(SLOTS)))
        steps.done(dve.scalar_tensor_tensor(base[:, :], first[:, :], float(P), self.ps[:, 1, :], ALU.mult, ALU.add))
        steps.done(dve.tensor_scalar(base[:, :], base[:, :], 1.0, None, ALU.subtract))
        for j in range(SLOT_COLS):
            for u in range(G):
                last = dve.tensor_scalar(self.cmp[:, j, u, :], first[:, :], s.iota_slot[:, j, u:u + 1], None, ALU.is_le)
        steps.done(dve.scalar_tensor_tensor(self.tail[:, :], first[:, :], -1.0, small[:, :], ALU.add, ALU.add))
        steps.done(dve.tensor_scalar(self.tail[:, :], self.tail[:, :], 0.0, s.lane_row[self.row], ALU.max, ALU.add))
        dve.tensor_copy(self.tail_i[:, :], self.tail[:, :])
        steps.done(dve.tensor_reduce(self.tile_f[:, :, :], self.cmp[:, :, :, 1:TILES], AX_X, ALU.add))
        dve.tensor_copy(self.tile_i[:, :, :], self.tile_f[:, :, :]).then_inc(tiles_ready, 1)

    def place_step(self, dve, s, key, t, n, steps):
        match, cum, term, pos = self.match, self.cum, self.term, self.pos
        if n == 0:
            steps.done(dve.tensor_scalar(match[:, :], key, s.iota[:, bass.ds(t, 1)], None, ALU.is_equal))
        if n == 1:
            steps.done(dve.tensor_tensor_scan(cum[:, :], match[:, :], self.none[:, :], 0.0, ALU.add, ALU.add))
        if n == 2:
            steps.done(dve.scalar_tensor_tensor(term[:, :], cum[:, :], self.base[:, bass.ds(t, 1)], match[:, :], ALU.add, ALU.mult))
        if n == 3:
            steps.done(dve.tensor_tensor(pos[:, :], pos[:, :], term[:, :], ALU.add))

    def finish(self, dve, steps):
        cell, rows = self.cell, self.rows
        steps.done(dve.tensor_copy(cell[:, :], self.pos[:, :]))
        steps.done(dve.tensor_scalar(rows[:, :], cell[:, :], P - 1, None, ALU.bitwise_and))
        steps.done(dve.tensor_scalar(cell[:, :], cell[:, :], 7, None, ALU.logical_shift_right))
        dve.tensor_copy(self.pos[:, :], rows[:, :])
        steps.done(dve.tensor_copy(self.cum[:, :], cell[:, :]))
        steps.done(dve.scalar_tensor_tensor(self.term[:, :], self.pos[:, :], float(self.row), self.cum[:, :], ALU.mult, ALU.add))
        steps.done(dve.tensor_copy(rows[:, :], self.term[:, :]))


def rank_phase(nc, s, d, ranks):
    with Phase(nc) as ctx:
        s_step = ctx.semaphore("rank1_step")
        s_count = ctx.semaphore("rank1_count")
        s_sums = ctx.semaphore("rank1_sums")
        s_tile = ctx.semaphore("rank1_tile")
        s_out = ctx.semaphore("rank1_out")
        s_back = ctx.semaphore("rank1_back")
        s_fill = ctx.semaphore("rank1_fill")
        s_zero = ctx.semaphore("rank1_zero")
        s_tails = ctx.semaphore("rank1_tails")
        key = s.tile_d[:, :]
        with nc.Block() as block:
            @block.vector
            def _(dve):
                steps = Steps(dve, s_step)
                ranks.clear(dve, steps)
                at = steps.n
                with dve.Fori(0, BUCKETS) as t:
                    ranks.count_bucket(dve, s, key, t, Steps(dve, s_step, t * 2 + at))
                steps.n = at + 2 * BUCKETS
                dve.sem_inc(s_count, 1)
                dve.wait_ge(s_sums, 1)
                ranks.bases(dve, s, steps, s_tile)
                at = steps.n
                with dve.Fori(0, BUCKETS) as t:
                    steps_t = Steps(dve, s_step, t * 4 + at)
                    for n in range(4):
                        ranks.place_step(dve, s, key, t, n, steps_t)
                steps.n = at + 4 * BUCKETS
                ranks.finish(dve, steps)

            @block.tensor
            def _(pe):
                pe.wait_ge(s_count, 1)
                ranks.sums(pe, s, s_sums)

            @block.sync
            def _(sp):
                fill_free(sp, d.sorted1, s.sentinel1, s_fill)
                sp.dma_start(d.zeros.rearrange("(p a) -> p a", p=P), s.zeros[:, 0:U * ATTR]).then_inc(s_zero, 16)
                sp.wait_ge(s_tile, 1)
                put_tiles(sp, d.chunk_tile1, ranks, s_out)
                sp.wait_ge(s_out, 16)
                sp.dma_start(s.chunk_tile_i[:, :], row_of(d.chunk_tile1[0:SLOTS]).broadcast_to([P, SLOTS])).then_inc(s_back, 16)
                sp.wait_ge(s_back, 16)
                sp.wait_ge(s_zero, 16)

            @block.gpsimd
            def _(pool):
                pool.wait_ge(s_fill, 16)
                pool.wait_ge(s_tile, 1)
                fill_tails(pool, d.sorted1, s.sentinel1, ranks, s_tails)


def fill_free(eng, dram, tile, done):
    eng.dma_start(dram.rearrange("(p k) w -> p k w", p=P)[:, FREE_FROM:SLOTS, :], tile[:, :, :]).then_inc(done, 16)


def fill_tails(pool, dram, tile, ranks, done):
    for t in range(TILES):
        pool.indirect_dma_start(dram, bass.IndirectOffsetOnAxis(ap=ranks.tail_i[:, t:t + 1], axis=0), tile[:, 0, :], None).then_inc(done, 16)
    pool.wait_ge(done, 16 * TILES)


def put_tiles(sp, chunk_tile, ranks, done):
    sp.dma_start(chunk_tile.rearrange("(j p u) -> p j u", p=P, u=G), ranks.tile_i[:, :, :]).then_inc(done, 16)


def sort_phase(nc, s, d, rows):
    with Phase(nc) as ctx:
        sb = lambda n, shape, dt=F32: ctx.enter_context(nc.sbuf_tensor(n, shape, dt))
        sem = lambda n: ctx.semaphore(n)
        w1_raw = sb("w1_raw", [F, ATTR])
        w2_raw = sb("w2_raw", [F, F])
        w1_t = sb("w1_t", [ATTR, F])
        w2_t = sb("w2_t", [F, F])
        b1 = sb("b1c", [F, 1])
        b2 = sb("b2r", [P, F])
        attr = [sb(f"attr{h}", [P, U, ATTR]) for h in range(2)]
        attr_t = sb("attr_t", [ATTR, U * P])
        act_t = sb("act_t", [F, U * P])
        edge = [sb(f"edge_{h}", [P, U, EDGE]) for h in range(2)]
        at = [sb(f"at_{h}", [P, U], I32) for h in range(2)]
        tr_ps = ctx.enter_context(nc.psum_tensor("attr_ps", [P, U * P], F32))
        z_ps = ctx.enter_context(nc.psum_tensor("z_ps", [P, U * P], F32))
        g_ps = ctx.enter_context(nc.psum_tensor("gate_ps", [P, U, 64], F32))
        s_w = sem("sort_w")
        s_wt = sem("sort_wt")
        s_wc = sem("sort_wc")
        s_zero = sem("sort_zero")
        s_tail = sem("sort_tail")
        s_attr = [sem(f"sort_attr{h}") for h in range(2)]
        s_turned = sem("sort_turned")
        s_attr_t = sem("sort_attr_t")
        s_z = sem("sort_z")
        s_act = sem("sort_act")
        s_gate = sem("sort_gate")
        s_gated = sem("sort_gated")
        s_go = sem("sort_go")
        s_pe_go = sem("sort_pe_go")
        s_sent = [sem(f"sort_sent{h}") for h in range(2)]
        with nc.Block() as block:
            @block.sync
            def _(sp):
                sp.dma_start(w1_raw[:, :], d.L2_gnn_W1).then_inc(s_w, 16)
                sp.dma_start(w2_raw[:, :], d.L2_gnn_W2).then_inc(s_w, 16)
                sp.dma_start(b1[:, :], column(d.L2_gnn_b1)).then_inc(s_w, 16)
                sp.dma_start(b2[:, :], row_of(d.L2_gnn_b2).broadcast_to([P, F])).then_inc(s_w, 16)
                sp.sem_inc(s_turned, 1)
                sp.sem_inc(s_turned, 1)
                with sp.Fori(0, PAIRS - 1) as i:
                    for h in range(2):
                        sp.wait_ge(s_turned, i * 2 + (h + 1))
                        sp.dma_start(attr[h][:, :, :], d.edge_attr_40[bass.ds(i * (2 * GROUP) + h * GROUP, GROUP), :].rearrange(
                            "(p u) f -> p u f", u=U)).then_inc(s_attr[h], 16)
                cut = FULL * GROUP + TAIL_P * U
                for h in range(2):
                    sp.wait_ge(s_turned, 2 * (PAIRS - 1) + h + 1)
                    ins = sp.dma_start(attr[h][:, :, :].rearrange("p u f -> p (u f)"), d.zeros.rearrange("(p a) -> p a", p=P))
                    if h == 0:
                        ins.then_inc(s_zero, 16)
                        sp.wait_ge(s_zero, 16)
                        sp.dma_start(attr[0][0:TAIL_P, :, :], d.edge_attr_40[FULL * GROUP:cut, :].rearrange("(p u) f -> p u f", u=U)).then_inc(s_tail, 16)
                        sp.wait_ge(s_tail, 16)
                        ins = sp.dma_start(attr[0][TAIL_P:TAIL_P + 1, 0:TAIL_U, :], d.edge_attr_40[cut:E, :].rearrange("(p u) f -> p u f", u=TAIL_U))
                    ins.then_inc(s_attr[h], 16)

            @block.tensor
            def _(pe):
                pe.wait_ge(s_w, 64)
                pe.transpose(tr_ps[0:ATTR, 0:F], w1_raw[:, :], s.ident[0:F, 0:F])
                pe.transpose(tr_ps[0:F, F:2 * F], w2_raw[:, :], s.ident[0:F, 0:F]).then_inc(s_wt, 1)
                pe.wait_ge(s_wc, 2)

                def turn_attributes(i, h):
                    pe.wait_ge(s_attr[h], i * 16 + 16)
                    pe.wait_ge(s_attr_t, i * 2 + (h + 1))
                    pe.sem_inc(s_pe_go, 1)
                    for u in range(U):
                        last = pe.transpose(tr_ps[0:ATTR, u * P:(u + 1) * P], attr[h][:, u, :], s.ident[:, :])
                    last.then_inc(s_turned, 1)

                def pair(i, final):
                    for h in range(2):
                        g = i * 2 + h
                        pe.wait_ge(s_attr_t, g + 2)
                        pe.wait_ge(s_act, g + 1)
                        pe.sem_inc(s_pe_go, 1)
                        for c in range(0, U * P, 512):
                            last = pe.matmul(z_ps[0:F, c:c + 512], w1_t[:, :], attr_t[:, c:c + 512], start=True, stop=True)
                        last.then_inc(s_z, 1)
                        if h == 0:
                            turn_attributes(i, 1)
                        elif not final:
                            turn_attributes(i + 1, 0)
                        pe.wait_ge(s_act, g + 2)
                        pe.wait_ge(s_gated, g + 1)
                        pe.sem_inc(s_pe_go, 1)
                        for u in range(U):
                            last = pe.matmul(g_ps[:, u, 0:F], act_t[:, u * P:(u + 1) * P], w2_t[:, :], start=True, stop=True)
                        last.then_inc(s_gate, 1)
                turn_attributes(0, 0)
                with pe.Fori(0, PAIRS - 1) as i:
                    pair(i, False)
                pair(PAIRS - 1, True)

            @block.scalar
            def _(act):
                act.wait_ge(s_wt, 1)
                act.copy(w1_t[:, :], tr_ps[0:ATTR, 0:F]).then_inc(s_wc, 1)
                act.copy(w2_t[:, :], tr_ps[0:F, F:2 * F]).then_inc(s_wc, 1)
                for seeded in (s_attr_t, s_act, s_gate, s_z):
                    act.sem_inc(seeded, 1)
                with act.Fori(0, PAIRS) as i:
                    for h in range(2):
                        g = i * 2 + h
                        act.wait_ge(s_turned, g + 3)
                        act.wait_ge(s_z, g + 1)
                        act.copy(attr_t[:, :], tr_ps[0:ATTR, :]).then_inc(s_attr_t, 1)
                        act.wait_ge(s_z, g + 2)
                        act.wait_ge(s_gate, g + 1)
                        act.activation(act_t[:, :], z_ps[0:F, :], ACT.Silu, bias=b1[:, 0:1]).then_inc(s_act, 1)

            @block.vector
            def _(dve):
                dve.sem_inc(s_gated, 1)
                dve.wait_ge(s_w, 64)
                with dve.Fori(0, PAIRS) as i:
                    for h in range(2):
                        g = i * 2 + h
                        k = i * (2 * U) + h * U
                        dve.wait_ge(s_sent[h], i * (16 * U) + 16)
                        dve.tensor_copy(edge[h][:, :, F:EDGE], s.meta[:, bass.ds(k, U), :])
                        dve.tensor_copy(at[h][:, :], rows[:, bass.ds(k, U)])
                        dve.wait_ge(s_gate, g + 2)
                        dve.tensor_tensor(edge[h][:, :, 0:F], g_ps[:, :, 0:F], mid(b2[:, :], U), ALU.add).then_inc(s_gated, 1)

            @block.gpsimd
            def _(pool):
                for h in range(2):
                    pool.dma_start(edge[h][:, 0, :], d.zeros.rearrange("(p a) -> p a", p=P)[:, 0:EDGE]).then_inc(s_sent[h], 16)
                with pool.Fori(0, PAIRS) as i:
                    for h in range(2):
                        pool.wait_ge(s_gated, i * 2 + (h + 2))
                        pool.sem_inc(s_go, 1)
                        for u in range(U):
                            pool.indirect_dma_start(d.sorted1, bass.IndirectOffsetOnAxis(ap=at[h][:, u:u + 1], axis=0),
                                                    edge[h][:, u, :], None).then_inc(s_sent[h], 16)
                for h in range(2):
                    pool.wait_ge(s_sent[h], PAIRS * 16 * U + 16)


def open_sums(pe, s, acc):
    for b in range(0, 32, 8):
        pe.matmul(acc[:, b:b + 8, :], s.zeros_b[:, 0:P], s.zeros_b[:, :], start=True, stop=False, skip_group_check=True)


def close_sums(dve, s, acc, used):
    for b in range(0, TILES, 8):
        n = min(8, TILES - b)
        dve.tensor_copy(s.agg[:, b:b + n, 0:used], acc[:, b:b + n, 0:used])


def load_tiles(s, pe, chunk_tile, first, h, buffers=1):
    pe.reg_load(s.tile_regs[h * G:(h + buffers) * G], chunk_tile[0:1, bass.ds(first, buffers * G)])
    return loaded_tiles(s, pe, h, buffers)


def loaded_tiles(s, pe, h, buffers=1):
    return [pe.snap(r, min_val=0, max_val=TILES - 1) for r in s.tile_regs[h * G:(h + buffers) * G]]


def edge_pass(nc, s, d, name, table, width, used, index, weight=None, ranks=None,
              find_max=False, join_max=False, adapt=False, edge_max=False):
    with Phase(nc) as ctx:
        sb = lambda n, shape, dt=F32: ctx.enter_context(nc.sbuf_tensor(f"{name}_{n}", shape, dt))
        ring = lambda n, shape, dt=F32: [sb(f"{n}{h}", shape, dt) for h in range(H)]
        sems = lambda n: [ctx.semaphore(f"{name}_{n}{h}") for h in range(H)]
        stage = ring("stage", [P, G], I32)
        rows = ring("rows", [P, G, width])
        scaled = ring("scaled", [P, G, width]) if weight is not None else rows
        onehot = ring("onehot", [P, G, P])
        masked = ring("masked", [P, G, P]) if find_max or edge_max else None
        line = sb("line", [P, SLOTS]) if join_max else None
        acc = ctx.enter_context(nc.psum_tensor(f"{name}_acc", [P, 32, 64], F32))
        if find_max or edge_max:
            side = [ctx.enter_context(nc.psum_tensor(f"{name}_side{h}", [P, G, P], F32)) for h in range(H)]
        if adapt:
            onehot_b = ring("onehot_b", [P, G, P], BF16)
            turned = ring("turned", [P, G, P])
            prod = ring("prod", [P, G, GDIM])
            turn_ps = ctx.enter_context(nc.psum_tensor(f"{name}_turn", [P, H, G, P], BF16))
            q_ps = ctx.enter_context(nc.psum_tensor(f"{name}_q", [P, 2, 8, 64], F32))
        s_staged, s_rows, s_scaled, s_onehot, s_added = sems("staged"), sems("rows"), sems("scaled"), sems("onehot"), sems("added")
        s_masked, s_side, s_side_read = sems("masked"), sems("side"), sems("side_read")
        s_narrow, s_turned, s_copied, s_q, s_q_read = sems("narrow"), sems("turned"), sems("copied"), sems("q"), sems("q_read")
        s_go = ctx.semaphore(f"{name}_go")
        s_step = ctx.semaphore(f"{name}_step")
        s_sum = ctx.semaphore(f"{name}_sum")
        s_loading = ctx.semaphore(f"{name}_loading")
        s_clear = ctx.semaphore(f"{name}_clear")
        ready, per = (s_scaled, 1) if weight is not None else (s_rows, 16 * G)
        at = lambda i, ahead, h: i * (H * G) + (ahead * H + h) * G
        with nc.Block() as block:
            if find_max:
                @block.sync
                def _(sp):
                    fields = d.sorted1.rearrange("(p k) w -> p k w", p=P)[:, :, F:EDGE]
                    sp.sem_inc(s_loading, 1)
                    with sp.Fori(0, TURNS) as i:
                        k = at(i, 0, 0)
                        sp.wait_ge(s_loading, i * 16 + 1)
                        sp.dma_start(s.edge[:, bass.ds(k, H * G), :], fields[:, bass.ds(k, H * G), :]).then_inc(s_loading, 16)

            @block.scalar
            def _(act):
                def stage_indices(i, ahead, h):
                    if find_max:
                        act.wait_ge(s_loading, i * 16 + (ahead * 16 + 17))
                    act.copy(stage[h][:, :], index[:, bass.ds(at(i, ahead, h), G)]).then_inc(s_staged[h], 1)

                def copy_turned(i, ahead, h):
                    if adapt:
                        act.wait_ge(s_turned[h], i + (ahead + 1))
                        act.wait_ge(s_q[h], i + (ahead + 1))
                        act.copy(turned[h][:, :, :], turn_ps[:, h, :, :]).then_inc(s_copied[h], 1)

                def turn(i, last):
                    for h in range(H):
                        if not last or h < H - 1:
                            copy_turned(i, (h + 1) // H, (h + 1) % H)
                        if not last:
                            act.wait_ge(s_added[h], i + 2)
                            if adapt:
                                act.wait_ge(s_q_read[h], i + 2)
                            stage_indices(i, 1, h)
                for h in range(H):
                    act.sem_inc(s_added[h], 1)
                    stage_indices(0, 0, h)
                copy_turned(0, 0, 0)
                with act.Fori(0, TURNS - 1) as i:
                    turn(i, False)
                turn(TURNS - 1, True)

            @block.gpsimd
            def _(pool):
                with pool.Fori(0, TURNS) as i:
                    for h in range(H):
                        pool.wait_ge(s_staged[h], i + 1)
                        pool.sem_inc(s_go, 1)
                        for u in range(G):
                            pool.indirect_dma_start(rows[h][:, u, :], None, table,
                                                    bass.IndirectOffsetOnAxis(ap=stage[h][:, u:u + 1], axis=0)).then_inc(s_rows[h], 16)

            @block.vector
            def _(dve):
                steps_ahead = 1 if find_max or edge_max else 0
                steps_turn = ((1 if find_max or edge_max else 0) + (1 if adapt else 0)) * H + (5 if join_max else 0) + (4 if edge_max else 0)

                def before_rows(i, ahead, h, steps):
                    k = at(i, ahead, h)
                    dve.wait_ge(s_added[h], i + (ahead + 1))
                    if find_max:
                        dve.wait_ge(s_loading, i * 16 + (ahead * 16 + 17))
                    for u in range(G):
                        last = dve.tensor_scalar(onehot[h][:, u, :], s.iota[:, :], s.edge[:, bass.ds(k + u, 1), LANE_D], None, ALU.is_equal)
                    last.then_inc(s_onehot[h], 1)
                    if adapt:
                        for u in range(G):
                            last = dve.tensor_scalar(onehot_b[h][:, u, :], s.iota_b[:, :], s.edge[:, bass.ds(k + u, 1), LANE_D], None, ALU.is_equal)
                        last.then_inc(s_narrow[h], 1)
                    if find_max:
                        dve.wait_ge(s_onehot[h], i + (ahead + 1))
                        steps.done(dve.tensor_scalar(masked[h][:, :, :], onehot[h][:, :, :], BIG, -BIG, ALU.mult, ALU.add))
                        dve.tensor_tensor(masked[h][:, :, :], masked[h][:, :, :], bc(s.edge[:, bass.ds(k, G), WEIGHT], P),
                                          ALU.add).then_inc(s_masked[h], 1)

                def read_side(i, ahead, h, steps):
                    k = at(i, ahead, h)
                    if find_max:
                        dve.wait_ge(s_side[h], i + (ahead + 1))
                        dve.tensor_reduce(s.top[:, bass.ds(k, G)], side[h][:, :, :], AX_X, ALU.max).then_inc(s_side_read[h], 1)
                    if edge_max:
                        dve.wait_ge(s_side[h], i + (ahead + 1))
                        dve.wait_ge(s_onehot[h], i + (ahead + 1))
                        dve.tensor_tensor(masked[h][:, :, :], onehot[h][:, :, :], side[h][:, :, :], ALU.mult).then_inc(s_side_read[h], 1)
                        dve.wait_ge(s_side_read[h], i + (ahead + 2))
                        steps.done(dve.tensor_reduce(s.edge_top[:, bass.ds(k, G)], masked[h][:, :, :], AX_X, ALU.add))

                def after_rows(i, h, steps):
                    k = at(i, 0, h)
                    if weight is not None:
                        dve.wait_ge(s_rows[h], i * (16 * G) + 16 * G)
                        dve.tensor_tensor(scaled[h][:, :, 0:used], rows[h][:, :, 0:used], bc(weight[:, bass.ds(k, G)], used),
                                          ALU.mult).then_inc(s_scaled[h], 1)
                    if adapt:
                        dve.wait_ge(s_q[h], i + 2)
                        dve.wait_ge(s_rows[h], i * (16 * G) + 16 * G)
                        dve.tensor_copy(s.mult[:, bass.ds(k, G)], q_ps[:, h % 2, 0:G, GDIM])
                        dve.tensor_tensor(prod[h][:, :, :], q_ps[:, h % 2, 0:G, 0:GDIM], rows[h][:, :, F + 1:F + 1 + GDIM], ALU.mult).then_inc(s_q_read[h], 1)
                        dve.wait_ge(s_q_read[h], i + 2)
                        steps.done(dve.tensor_reduce(s.adapt[:, bass.ds(k, G)], prod[h][:, :, :], AX_X, ALU.add))

                def turn(i, last):
                    steps = Steps(dve, s_step, i * steps_turn + steps_ahead)
                    for h in range(H):
                        if not last or h < H - 1:
                            before_rows(i, (h + 1) // H, (h + 1) % H, steps)
                        after_rows(i, h, steps)
                        if not last or h < H - 1:
                            read_side(i, (h + 1) // H, (h + 1) % H, steps)
                        if edge_max:
                            ranks.place_step(dve, s, s.tile_s[:, :], i, h, steps)
                        if join_max and h == 0:
                            steps.done(dve.tensor_scalar(line[:, :], s.chunk_tile[:, :], s.iota[:, bass.ds(i, 1)], -BIG, ALU.not_equal, ALU.mult))
                        if join_max and h == 1:
                            steps.done(dve.tensor_tensor(line[:, :], line[:, :], s.top[:, :], ALU.add))
                        if join_max and h == 2:
                            steps.done(dve.tensor_reduce(s.seg_max[:, bass.ds(i, 1)], line[:, :], AX_X, ALU.max))
                        if join_max and h == 3:
                            ranks.count_bucket(dve, s, s.tile_s[:, :], i, steps)
                if adapt:
                    for h in range(H):
                        dve.sem_inc(s_q_read[h], 1)
                if find_max:
                    ranks.clear(dve, Steps(dve, s_clear))
                    dve.memset(s.edge_top[:, :], 0.0)
                    dve.tensor_copy(s.chunk_tile[:, :], s.chunk_tile_i[:, :])
                ahead_steps = Steps(dve, s_step)
                before_rows(0, 0, 0, ahead_steps)
                read_side(0, 0, 0, ahead_steps)
                with dve.Fori(0, TURNS - 1) as i:
                    turn(i, False)
                turn(TURNS - 1, True)
                if find_max:
                    dve.tensor_copy(s.tile_s[:, :], s.edge[:, :, TILE_S])
                dve.wait_ge(s_sum, 1)
                close_sums(dve, s, acc, used)

            @block.tensor
            def _(pe):
                def before_rows(i, ahead, h):
                    tiles = load_tiles(s, pe, s.chunk_tile_i, at(i, ahead, h), h)
                    if find_max:
                        pe.wait_ge(s_masked[h], i + (ahead + 1))
                        pe.wait_ge(s_side_read[h], i + (ahead + 1))
                        for u in range(G):
                            last = pe.transpose(side[h][:, u, :], masked[h][:, u, :], s.ident[:, :])
                        last.then_inc(s_side[h], 1)
                    if edge_max:
                        pe.wait_ge(s_side_read[h], i + (ahead + 1))
                        for u in range(G):
                            last = pe.matmul(side[h][:, u, :], s.ident[:, :], s.max_rows[:, bass.ds(tiles[u] * P, P)],
                                             start=True, stop=True)
                        last.then_inc(s_side[h], 1)
                    if adapt:
                        pe.wait_ge(s_narrow[h], i + (ahead + 1))
                        pe.wait_ge(s_copied[h], i + (ahead + 1))
                        for u in range(G):
                            last = pe.transpose(turn_ps[:, h, u, :], onehot_b[h][:, u, :], s.ident_b[:, :])
                        last.then_inc(s_turned[h], 1)
                    return tiles

                def spread_nodes(i, ahead, h, tiles):
                    if adapt:
                        pe.wait_ge(s_copied[h], i + (ahead + 2))
                        pe.wait_ge(s_q_read[(h + 2) % H], i + (ahead + h // 2 + 1))
                        for u in range(G):
                            last = pe.matmul(q_ps[:, h % 2, u, 0:GDIM + 1], turned[h][:, u, :], s.qnode[:, bass.ds(tiles[u], 1), :],
                                             start=True, stop=True)
                        last.then_inc(s_q[h], 1)

                def turn(i, last_turn):
                    following = loaded_tiles(s, pe, 0)
                    for h in range(H):
                        tiles = following
                        if not last_turn or h < H - 1:
                            following = before_rows(i, (h + 1) // H, (h + 1) % H)
                        pe.wait_ge(ready[h], i * per + per)
                        pe.wait_ge(s_onehot[h], i + 1)
                        for u in range(G):
                            last = pe.matmul(acc[:, bass.ds(tiles[u], 1), 0:used], onehot[h][:, u, :],
                                             scaled[h][:, u, 0:used], start=False, stop=False, skip_group_check=True)
                        last.then_inc(s_added[h], 1)
                        if not last_turn or h < H - 1:
                            spread_nodes(i, (h + 1) // H, (h + 1) % H, following)
                for h in range(H):
                    if find_max or edge_max:
                        pe.sem_inc(s_side_read[h], 1)
                    if adapt:
                        pe.sem_inc(s_q[h], 1)
                        pe.sem_inc(s_copied[h], 1)
                open_sums(pe, s, acc)
                spread_nodes(0, 0, 0, before_rows(0, 0, 0))
                with pe.Fori(0, TURNS - 1) as i:
                    turn(i, False)
                turn(TURNS - 1, True)
                pe.drain().then_inc(s_sum, 1)


def send_pass(nc, s, d, rows2):
    with Phase(nc) as ctx:
        sb = lambda n, shape, dt=F32: ctx.enter_context(nc.sbuf_tensor(f"send_{n}", shape, dt))
        ring = lambda n, shape, dt=F32: [sb(f"{n}{h}", shape, dt) for h in range(H)]
        sems = lambda n: [ctx.semaphore(f"send_{n}{h}") for h in range(H)]
        stage = ring("stage", [P, G], I32)
        gate = ring("gate", [P, G, F])
        msg = ring("msg", [P, G, MSG])
        onehot_b = ring("onehot_b", [P, G, P], BF16)
        turned = ring("turned", [P, G, P])
        coef = sb("coef", [P, SLOTS])
        turn_ps = [ctx.enter_context(nc.psum_tensor(f"send_turn{h}", [P, G, P], BF16)) for h in range(H)]
        h_ps = [ctx.enter_context(nc.psum_tensor(f"send_h{h}", [P, G, 64], F32)) for h in range(H)]
        s_gate, s_staged, s_narrow, s_turned, s_copied, s_h, s_mixed, s_msg, s_sent = (
            sems(n) for n in ("gate", "staged", "narrow", "turned", "copied", "h", "mixed", "msg", "sent"))
        s_step = ctx.semaphore("send_step")
        s_go = ctx.semaphore("send_go")
        at = lambda i, ahead, h: i * (H * G) + (ahead * H + h) * G
        v = d.sorted1.rearrange("(p k) w -> p k w", p=P)
        with nc.Block() as block:
            @block.sync
            def _(sp):
                for h in range(H):
                    sp.sem_inc(s_msg[h], 1)
                with sp.Fori(0, TURNS) as i:
                    for h in range(H):
                        sp.wait_ge(s_msg[h], i + 1)
                        sp.dma_start(gate[h][:, :, :], v[:, bass.ds(at(i, 0, h), G), 0:F]).then_inc(s_gate[h], 16)

            @block.scalar
            def _(act):
                def copy_turned(i, ahead, h):
                    act.wait_ge(s_turned[h], i + (ahead + 2))
                    act.wait_ge(s_h[h], i + (ahead + 1))
                    act.copy(turned[h][:, :, :], turn_ps[h][:, :, :]).then_inc(s_copied[h], 1)

                def turn(i, last):
                    for h in range(H):
                        if not last or h < H - 1:
                            copy_turned(i, (h + 1) // H, (h + 1) % H)
                        act.wait_ge(s_sent[h], i * (16 * G) + 16)
                        act.copy(stage[h][:, :], rows2[:, bass.ds(at(i, 0, h), G)]).then_inc(s_staged[h], 1)
                        act.copy(msg[h][:, :, F], s.mult[:, bass.ds(at(i, 0, h), G)]).then_inc(s_staged[h], 1)
                        act.copy(msg[h][:, :, F + 1], s.edge[:, bass.ds(at(i, 0, h), G), LANE_S]).then_inc(s_staged[h], 1)
                copy_turned(0, 0, 0)
                with act.Fori(0, TURNS - 1) as i:
                    turn(i, False)
                turn(TURNS - 1, True)

            @block.gpsimd
            def _(pool):
                for h in range(H):
                    pool.dma_start(msg[h][:, :, :].rearrange("p g w -> p (g w)"),
                                   d.zeros.rearrange("(p a) -> p a", p=P)[:, 0:G * MSG]).then_inc(s_sent[h], 16)
                with pool.Fori(0, TURNS) as i:
                    for h in range(H):
                        pool.wait_ge(s_staged[h], i * 3 + 3)
                        pool.sem_inc(s_go, 1)
                        pool.wait_ge(s_msg[h], i + 2)
                        pool.sem_inc(s_go, 1)
                        for u in range(G):
                            pool.indirect_dma_start(d.sorted2, bass.IndirectOffsetOnAxis(ap=stage[h][:, u:u + 1], axis=0),
                                                    msg[h][:, u, :], None).then_inc(s_sent[h], 16)
                for h in range(H):
                    pool.wait_ge(s_sent[h], TURNS * 16 * G + 16)

            @block.vector
            def _(dve):
                steps = Steps(dve, s_step)
                steps.done(dve.tensor_tensor(coef[:, :], s.mult[:, :], s.edge[:, :, CUT], ALU.mult))

                def write_onehots(i, ahead, h):
                    dve.wait_ge(s_turned[h], i + (ahead + 1))
                    for u in range(G):
                        last = dve.tensor_scalar(onehot_b[h][:, u, :], s.iota_b[:, :], s.edge[:, bass.ds(at(i, ahead, h) + u, 1), LANE_D], None, ALU.is_equal)
                    last.then_inc(s_narrow[h], 1)

                def turn(i, last):
                    ordered = Steps(dve, s_step, i * H + 1)
                    for h in range(H):
                        k = at(i, 0, h)
                        if not last or h < H - 1:
                            write_onehots(i, (h + 1) // H, (h + 1) % H)
                        dve.wait_ge(s_gate[h], i * 16 + 16)
                        ordered.done(dve.tensor_tensor(gate[h][:, :, :], gate[h][:, :, :], bc(s.adapt[:, bass.ds(k, G)], F), ALU.add))
                        dve.wait_ge(s_h[h], i + 2)
                        dve.tensor_tensor(gate[h][:, :, :], gate[h][:, :, :], h_ps[h][:, :, 0:F], ALU.mult).then_inc(s_mixed[h], 1)
                        dve.wait_ge(s_mixed[h], i + 1)
                        dve.wait_ge(s_sent[h], i * (16 * G) + 16)
                        dve.tensor_tensor(msg[h][:, :, 0:F], gate[h][:, :, :], bc(coef[:, bass.ds(k, G)], F), ALU.mult).then_inc(s_msg[h], 1)
                for h in range(H):
                    dve.sem_inc(s_turned[h], 1)
                write_onehots(0, 0, 0)
                with dve.Fori(0, TURNS - 1) as i:
                    turn(i, False)
                turn(TURNS - 1, True)

            @block.tensor
            def _(pe):
                def features(i, h):
                    tiles = load_tiles(s, pe, s.chunk_tile_i, at(i, 0, h), h)
                    pe.wait_ge(s_narrow[h], i + 1)
                    for u in range(G):
                        last = pe.transpose(turn_ps[h][:, u, :], onehot_b[h][:, u, :], s.ident_b[:, :])
                    last.then_inc(s_turned[h], 1)
                    pe.wait_ge(s_copied[h], i + 1)
                    pe.wait_ge(s_msg[h], i + 1)
                    for u in range(G):
                        last = pe.matmul(h_ps[h][:, u, 0:F], turned[h][:, u, :], s.h[:, bass.ds(tiles[u], 1), :],
                                         start=True, stop=True)
                    last.then_inc(s_h[h], 1)
                for h in range(H):
                    pe.sem_inc(s_h[h], 1)
                with pe.Fori(0, TURNS) as i:
                    for h in range(H):
                        features(i, h)


def source_pass(nc, s, d):
    with Phase(nc) as ctx:
        sb = lambda n, shape, dt=F32: ctx.enter_context(nc.sbuf_tensor(f"source_{n}", shape, dt))
        ring = lambda n, shape, dt=F32: [sb(f"{n}{h}", shape, dt) for h in range(H)]
        sems = lambda n: [ctx.semaphore(f"source_{n}{h}") for h in range(H)]
        msg = ring("msg", [P, H * G, MSG])
        onehot = ring("onehot", [P, G, P])
        acc = ctx.enter_context(nc.psum_tensor("source_acc", [P, 32, 64], F32))
        s_msg, s_onehot, s_added = sems("msg"), sems("onehot"), sems("added")
        s_sum = ctx.semaphore("source_sum")
        v = d.sorted2.rearrange("(p k) w -> p k w", p=P)
        with nc.Block() as block:
            @block.sync
            def _(sp):
                with sp.Fori(0, TURNS // H) as i:
                    for b in range(H):
                        sp.wait_ge(s_added[H - 1], i * H + (b + 1))
                        sp.dma_start(msg[b][:, :, :], v[:, bass.ds(i * (H * H * G) + b * H * G, H * G), :]).then_inc(s_msg[b], 16)

            @block.vector
            def _(dve):
                with dve.Fori(0, TURNS // H) as i:
                    for b in range(H):
                        dve.wait_ge(s_msg[b], i * 16 + 16)
                        for h in range(H):
                            dve.wait_ge(s_added[h], i * H + (b + H))
                            for u in range(G):
                                k = h * G + u
                                last = dve.tensor_scalar(onehot[h][:, u, :], s.iota[:, :], msg[b][:, k, F + 1:F + 2], None, ALU.is_equal)
                            last.then_inc(s_onehot[h], 1)
                dve.wait_ge(s_sum, 1)
                close_sums(dve, s, acc, F + 1)

            @block.tensor
            def _(pe):
                for h in range(H):
                    pe.sem_inc(s_added[h], H)
                open_sums(pe, s, acc)
                with pe.Fori(0, TURNS // H) as i:
                    for b in range(H):
                        tiles = load_tiles(s, pe, s.source_tile, i * (H * H * G) + b * (H * G), 0, H)
                        pe.wait_ge(s_msg[b], i * 16 + 16)
                        for h in range(H):
                            pe.wait_ge(s_onehot[h], i * H + (b + 1))
                            for u in range(G):
                                k = h * G + u
                                last = pe.matmul(acc[:, bass.ds(tiles[k], 1), 0:F + 1], onehot[h][:, u, :],
                                                 msg[b][:, k, 0:F + 1], start=False, stop=False, skip_group_check=True)
                            last.then_inc(s_added[h], 1)
                pe.drain().then_inc(s_sum, 1)


def sage_phase(nc, s, d, layer, w_self, w_neigh, bias, ranks=None):
    with Phase(nc) as ctx:
        sb = lambda n, shape, dt=F32: ctx.enter_context(nc.sbuf_tensor(f"{layer}_{n}", shape, dt))
        sem = lambda n: ctx.semaphore(f"{layer}_{n}")
        both = sb("both", [P, TILES, 2 * F])
        w = sb("w", [2 * F, F])
        b = sb("b", [P, F])
        deg = sb("deg", [P, TILES])
        res = sb("res", [P, TILES, F])
        tmp = sb("tmp", [P, TILES, F])
        part = sb("part", [P, NG, 2 * F])
        part_t = sb("part_t", [2 * F, NG, P])
        t_ps = ctx.enter_context(nc.psum_tensor(f"{layer}_t", [P, 8, P], F32))
        o_ps = ctx.enter_context(nc.psum_tensor(f"{layer}_o", [P, NG, 64], F32))
        s_w = sem("s_w")
        s_step = sem("s_step")
        s_both = sem("s_both")
        s_part = sem("s_part")
        s_t = sem("s_t")
        s_tc = sem("s_tc")
        s_o = sem("s_o")
        s_res = sem("s_res")
        s_var = sem("s_var")
        s_std = sem("s_std")
        s_h = sem("s_h")
        s_out = sem("s_out")
        s_back = sem("s_back")
        s_sums = sem("s_sums")
        s_tile = sem("s_tile")
        first = layer == "sage1"
        with nc.Block() as block:
            @block.sync
            def _(sp):
                sp.dma_start(w[0:F, :], w_self).then_inc(s_w, 16)
                sp.dma_start(w[F:2 * F, :], w_neigh).then_inc(s_w, 16)
                sp.dma_start(b[:, :], row_of(bias).broadcast_to([P, F])).then_inc(s_w, 16)
                if first:
                    sp.wait_ge(s_h, 1)
                    put_table(sp, d.table, s.tab[:, :, 0:W0], W0, s_out)
                    sp.wait_ge(s_out, 16)
                else:
                    sp.dma_start(d.seg_max.rearrange("(t p) -> p t", p=P), s.seg_max[:, 0:TILES]).then_inc(s_out, 16)
                    sp.wait_ge(s_out, 16)
                    sp.dma_start(s.max_rows[:, :], row_of(d.seg_max).broadcast_to([P, NODES])).then_inc(s_back, 16)
                    sp.wait_ge(s_tile, 1)
                    put_tiles(sp, d.chunk_tile2, ranks, s_out)
                    sp.wait_ge(s_out, 32)
                    sp.dma_start(s.source_tile[:, :], row_of(d.chunk_tile2[0:SLOTS])).then_inc(s_back, 16)
                    sp.wait_ge(s_back, 32)

            @block.scalar
            def _(act):
                act.wait_ge(s_both, 1)
                with act.Fori(0, NTURNS) as i:
                    act.copy(part[:, :, :], both[:, bass.ds(i * NG, NG), :]).then_inc(s_part, 1)
                    act.wait_ge(s_t, i + 1)
                    act.copy(part_t[:, :, :], t_ps[0:2 * F, 0:NG, :]).then_inc(s_tc, 1)
                    act.wait_ge(s_o, i + 1)
                    act.sem_inc(s_part, 1)
                if not first:
                    layernorm_relu(None, act, s, None, None, None, s.stat, None, s_var, s_std, 1)

            @block.tensor
            def _(pe):
                if not first:
                    ranks.sums(pe, s, s_sums)
                pe.wait_ge(s_w, 48)
                with pe.Fori(0, NTURNS) as i:
                    pe.wait_ge(s_part, i * 2 + 1)
                    for j in range(NG):
                        last = pe.transpose(t_ps[0:2 * F, j, :], part[:, j, :], s.ident[:, :])
                    last.then_inc(s_t, 1)
                    pe.wait_ge(s_tc, i + 1)
                    pe.wait_ge(s_res, i + 1)
                    for j in range(NG):
                        last = pe.matmul(o_ps[:, j, 0:F], part_t[:, j, :], w[:, :], start=True, stop=True)
                    last.then_inc(s_o, 1)

            @block.vector
            def _(dve):
                steps = Steps(dve, s_step)
                dve.sem_inc(s_res, 1)
                steps.done(dve.tensor_scalar(deg[:, :], s.agg[:, :, F], 1.0, None, ALU.max))
                steps.done(dve.reciprocal(deg[:, :], deg[:, :]))
                dve.tensor_copy(both[:, :, 0:F], s.h[:, :, :])
                dve.tensor_tensor(both[:, :, F:], s.agg[:, :, 0:F], bc(deg[:, :], F), ALU.mult).then_inc(s_both, 1)
                if not first:
                    dve.wait_ge(s_sums, 1)
                    ranks.bases(dve, s, steps, s_tile)
                dve.wait_ge(s_w, 48)
                with dve.Fori(0, NTURNS) as i:
                    dve.wait_ge(s_o, i + 1)
                    dve.tensor_tensor(res[:, bass.ds(i * NG, NG), :], o_ps[:, :, 0:F], mid(b[:, :], NG), ALU.add).then_inc(s_res, 1)
                dve.wait_ge(s_res, NTURNS + 1)
                if first:
                    dve.tensor_scalar(s.h[:, :, :], res[:, :, :], 0.0, None, ALU.max)
                    dve.tensor_scalar(s.tab[:, :, 0:F], res[:, :, :], 0.0, None, ALU.max).then_inc(s_h, 1)
                else:
                    steps.done(dve.tensor_tensor(s.x[:, :, :], s.x[:, :, :], res[:, :, :], ALU.add))
                    layernorm_relu(dve, None, s, s.x[:, :, :], s.h[:, :, :], tmp[:, :, :], s.stat, steps, s_var, s_std, 1)


def relation_phase(nc, s, d, ranks):
    with Phase(nc) as ctx:
        sb = lambda n, shape, dt=F32: ctx.enter_context(nc.sbuf_tensor(f"rel_{n}", shape, dt))
        sem = lambda n: ctx.semaphore(f"rel_{n}")
        R2 = RELS // 2
        w1 = sb("w1", [F, RELS, F])
        w2 = sb("w2", [2 * F, R2, 2 * F])
        b1 = sb("b1", [2 * F, 1])
        part = sb("part", [P, NG, F])
        part_t = sb("part_t", [F, NG * P])
        hid = [sb(f"hid{m}", [2 * F, NG * P]) for m in range(R2)]
        out = [sb(f"out{m}", [P, RELS * F]) for m in range(NG)]
        t_ps = ctx.enter_context(nc.psum_tensor("rel_t", [P, 8, P], F32))
        z_ps = [ctx.enter_context(nc.psum_tensor(f"rel_z{m}", [P, 8 * P], F32)) for m in range(2)]
        o_ps = [ctx.enter_context(nc.psum_tensor(f"rel_o{m}", [P, 512], F32)) for m in range(2)]
        s_pe_go, s_fill, s_tails = sem("s_pe_go"), sem("s_fill"), sem("s_tails")
        s_blank, s_w, s_part, s_t, s_tc, s_z, s_hid, s_o, s_oc, s_out = (
            sem(n) for n in ("s_blank", "s_w", "s_part", "s_t", "s_tc", "s_z", "s_hid", "s_o", "s_oc", "s_out"))
        table = d.table_r.rearrange("(t p r) w -> t p (r w)", p=P, r=RELS)
        with nc.Block() as block:
            @block.sync
            def _(sp):
                sp.dma_start(w1[:, :, :], d.L1_gnn_weight1.rearrange("r i j -> i r j")).then_inc(s_w, 16)
                for k in range(2):
                    sp.dma_start(b1[k * F:(k + 1) * F, :], column(d.L1_gnn_bias1)).then_inc(s_w, 16)
                sp.wait_ge(s_blank, 1)
                for k in range(2):
                    sp.dma_start(w2[k * F:(k + 1) * F, :, k * F:(k + 1) * F],
                                 d.L1_gnn_weight2.rearrange("(m k) j o -> k j m o", k=2)[k]).then_inc(s_w, 16)
                sp.dma_start(out[0][:, 0:F], row_of(d.L1_gnn_bias1).broadcast_to([P, F])).then_inc(s_out, 16)
                with sp.Fori(0, NTURNS) as i:
                    for j in range(NG):
                        sp.wait_ge(s_oc, i * NG + (j + 2))
                        sp.dma_start(table[bass.ds(i * NG + j, 1), :, :].rearrange("a p w -> (a p) w"), out[j][:, :]).then_inc(s_out, 16)
                sp.wait_ge(s_out, 16 * TILES + 16)

            @block.gpsimd
            def _(pool):
                fill_free(pool, d.sorted2, s.sentinel2, s_fill)
                pool.wait_ge(s_fill, 16)
                fill_tails(pool, d.sorted2, s.sentinel2, ranks, s_tails)

            @block.scalar
            def _(act):
                act.sem_inc(s_hid, 1)
                act.sem_inc(s_hid, 1)
                act.wait_ge(s_w, 80)
                with act.Fori(0, NTURNS) as i:
                    act.wait_ge(s_t, i + 1)
                    act.copy(part[:, :, :], s.h[:, bass.ds(i * NG, NG), :]).then_inc(s_part, 1)
                    act.wait_ge(s_t, i + 2)
                    act.wait_ge(s_z, i * R2 + 1)
                    act.copy(part_t[:, :], t_ps[0:F, 0:NG, :].rearrange("p g n -> p (g n)")).then_inc(s_tc, 1)
                    act.wait_ge(s_o, i * NG + 1)
                    for m in range(R2):
                        act.wait_ge(s_z, i * R2 + (m + 2))
                        act.activation(hid[m][:, :], z_ps[m % 2][0:2 * F, 0:NG * P], ACT.Relu, bias=b1[:, 0:1]).then_inc(s_hid, 1)

            @block.tensor
            def _(pe):
                pe.sem_inc(s_t, 1)
                pe.sem_inc(s_z, 1)
                pe.sem_inc(s_o, 1)
                pe.wait_ge(s_w, 80)
                with pe.Fori(0, NTURNS) as i:
                    pe.wait_ge(s_part, i + 1)
                    pe.sem_inc(s_pe_go, 1)
                    for j in range(NG):
                        last = pe.transpose(t_ps[0:F, j, :], part[:, j, :], s.ident[:, :])
                    last.then_inc(s_t, 1)
                    pe.wait_ge(s_tc, i + 1)
                    for m in range(R2):
                        pe.wait_ge(s_hid, i * R2 + (m + 1))
                        pe.sem_inc(s_pe_go, 1)
                        for c, n in ((0, 512), (512, NG * P - 512)):
                            last = pe.matmul(z_ps[m % 2][0:2 * F, c:c + n], w1[:, 2 * m:2 * m + 2, :].rearrange("i r j -> i (r j)"),
                                             part_t[:, c:c + n], start=True, stop=True)
                        last.then_inc(s_z, 1)
                    pe.wait_ge(s_hid, i * R2 + (R2 + 2))
                    for j in range(NG):
                        pe.wait_ge(s_oc, i * NG + (j + 1))
                        for m in range(R2):
                            last = pe.matmul(o_ps[j % 2][:, m * 2 * F:(m + 1) * 2 * F], hid[m][:, j * P:(j + 1) * P], w2[:, m, :],
                                             start=True, stop=True)
                        last.then_inc(s_o, 1)

            @block.vector
            def _(dve):
                dve.memset(w2[:, :, :], 0.0).then_inc(s_blank, 1)
                dve.sem_inc(s_oc, 1)
                with dve.Fori(0, NTURNS) as i:
                    dve.wait_ge(s_out, i * (16 * NG) + 16)
                    for j in range(NG):
                        dve.wait_ge(s_o, i * NG + (j + 2))
                        dve.tensor_copy(out[j][:, :], o_ps[j % 2][:, 0:RELS * F]).then_inc(s_oc, 1)


def join_phase(nc, s, d, name, stage, ranks=None):
    with Phase(nc) as ctx:
        sb = lambda n, shape, dt=F32: ctx.enter_context(nc.sbuf_tensor(f"{name}_{n}", shape, dt))
        sem = lambda n: ctx.semaphore(f"{name}_{n}")
        rows = sb("rows", [P, 2, F])
        tmp = sb("tmp", [P, TILES, F])
        y = sb("y", [P, TILES, F])
        shift = sb("shift", [P, SLOTS]) if stage == "relation" else None
        den = sb("den", [P, TILES])
        s_w, s_step, s_var, s_std, s_h, s_out, s_arg, s_exp = (
            sem(n) for n in ("s_w", "s_step", "s_var", "s_std", "s_h", "s_out", "s_arg", "s_exp"))
        vectors = {"relation": [d.L1_gnn_bias2], "gated": [d.L2_gnn_gamma, d.L2_gnn_beta], "softmax": []}[stage]
        with nc.Block() as block:
            @block.sync
            def _(sp):
                for n, vec in enumerate(vectors):
                    sp.dma_start(rows[:, n, :], row_of(vec).broadcast_to([P, F])).then_inc(s_w, 16)
                if stage != "relation":
                    sp.wait_ge(s_h, 1)
                if stage == "gated":
                    put_table(sp, d.table, s.tab[:, :, 0:W0], W0, s_out)
                    sp.wait_ge(s_out, 16)
                if stage == "softmax":
                    sp.dma_start(node_rows(d.out, 0, P, 0, TILES - 1), y[:, 0:TILES - 1, :]).then_inc(s_out, 16)
                    sp.dma_start(d.out[(TILES - 1) * P:N, :], y[0:LAST, TILES - 1, :]).then_inc(s_out, 16)
                    sp.wait_ge(s_out, 32)

            @block.scalar
            def _(act):
                if stage == "relation":
                    act.wait_ge(s_arg, 1)
                    act.activation(s.ex[:, :], shift[:, :], ACT.Exp).then_inc(s_exp, 1)
                if stage == "softmax":
                    act.wait_ge(s_arg, 1)
                    act.activation(tmp[:, :, :], tmp[:, :, :], ACT.Exp).then_inc(s_exp, 1)
                    return
                layernorm_relu(None, act, s, None, None, None, s.stat, None, s_var, s_std, 1)
                if stage == "gated":
                    layernorm_relu(None, act, s, None, None, None, s.stat, None, s_var, s_std, 2)

            @block.vector
            def _(dve):
                steps = Steps(dve, s_step)
                agg = s.agg[:, :, 0:F]
                if stage == "relation":
                    steps.done(dve.tensor_tensor(shift[:, :], s.edge[:, :, WEIGHT], s.edge_top[:, :], ALU.subtract))
                    dve.tensor_scalar(shift[:, :], shift[:, :], 0.0, None, ALU.min).then_inc(s_arg, 1)
                    dve.wait_ge(s_w, 16)
                    steps.done(dve.tensor_tensor(y[:, :, :], agg, mid(rows[:, 0, :], TILES), ALU.add))
                    steps.done(dve.scalar_tensor_tensor(s.x[:, :, :], y[:, :, :], 0.0, s.x[:, :, :], ALU.max, ALU.add))
                    layernorm_relu(dve, None, s, s.x[:, :, :], s.h[:, :, :], tmp[:, :, :], s.stat, steps, s_var, s_std, 1)
                    ranks.finish(dve, steps)
                    dve.wait_ge(s_exp, 1)
                elif stage == "gated":
                    steps.done(dve.tensor_scalar(den[:, :], s.agg[:, :, F], 1e-8, None, ALU.max))
                    steps.done(dve.reciprocal(den[:, :], den[:, :]))
                    steps.done(dve.tensor_tensor(tmp[:, :, :], agg, bc(den[:, :], F), ALU.mult))
                    steps.done(dve.tensor_tensor(s.h[:, :, :], s.h[:, :, :], tmp[:, :, :], ALU.add))
                    layernorm_relu(dve, None, s, s.h[:, :, :], y[:, :, :], tmp[:, :, :], s.stat, steps, s_var, s_std, 1, relu=False)
                    dve.wait_ge(s_w, 32)
                    steps.done(dve.tensor_tensor(y[:, :, :], y[:, :, :], mid(rows[:, 0, :], TILES), ALU.mult))
                    steps.done(dve.tensor_tensor(y[:, :, :], y[:, :, :], mid(rows[:, 1, :], TILES), ALU.add))
                    steps.done(dve.tensor_tensor(s.x[:, :, :], s.x[:, :, :], y[:, :, :], ALU.add))
                    layernorm_relu(dve, None, s, s.x[:, :, :], s.h[:, :, :], tmp[:, :, :], s.stat, steps, s_var, s_std, 2)
                    dve.tensor_copy(s.tab[:, :, 0:F], s.h[:, :, :]).then_inc(s_h, 1)
                else:
                    steps.done(dve.tensor_scalar(den[:, :], s.agg[:, :, F], 1.0, None, ALU.max))
                    steps.done(dve.reciprocal(den[:, :], den[:, :]))
                    steps.done(dve.tensor_tensor(y[:, :, :], agg, bc(den[:, :], F), ALU.mult))
                    dve.tensor_scalar(tmp[:, :, :], y[:, :, :], 0.0, None, ALU.min).then_inc(s_arg, 1)
                    steps.done(dve.tensor_scalar(y[:, :, :], y[:, :, :], 0.0, None, ALU.max))
                    steps.done(dve.tensor_tensor(s.x[:, :, :], s.x[:, :, :], y[:, :, :], ALU.add))
                    dve.wait_ge(s_exp, 1)
                    steps.done(dve.tensor_scalar(tmp[:, :, :], tmp[:, :, :], 1.0, None, ALU.subtract))
                    dve.tensor_tensor(y[:, :, :], s.x[:, :, :], tmp[:, :, :], ALU.add).then_inc(s_h, 1)


def build(nc, x, src, dst, edge_attr_40, edge_type_8, edge_weight, edge_weight1, node_type_119, node_vec, out,
          L0_gnn_W_self1, L0_gnn_W_neigh1, L0_gnn_b1, L0_gnn_W_self2, L0_gnn_W_neigh2, L0_gnn_b2,
          L1_gnn_weight1, L1_gnn_weight2, L1_gnn_bias1, L1_gnn_bias2,
          L2_gnn_W1, L2_gnn_b1, L2_gnn_W2, L2_gnn_b2, L2_gnn_emb, L2_gnn_adaptW, L2_gnn_gamma, L2_gnn_beta):
    s, d = Store(), Store()
    d.x = x
    d.src = src
    d.dst = dst
    d.edge_attr_40 = edge_attr_40
    d.edge_type_8 = edge_type_8
    d.edge_weight = edge_weight
    d.edge_weight1 = edge_weight1
    d.node_type_119 = node_type_119
    d.node_vec = node_vec
    d.L0_gnn_W_self1 = L0_gnn_W_self1
    d.L0_gnn_W_neigh1 = L0_gnn_W_neigh1
    d.L0_gnn_b1 = L0_gnn_b1
    d.L0_gnn_W_self2 = L0_gnn_W_self2
    d.L0_gnn_W_neigh2 = L0_gnn_W_neigh2
    d.L0_gnn_b2 = L0_gnn_b2
    d.L1_gnn_weight1 = L1_gnn_weight1
    d.L1_gnn_weight2 = L1_gnn_weight2
    d.L1_gnn_bias1 = L1_gnn_bias1
    d.L1_gnn_bias2 = L1_gnn_bias2
    d.L2_gnn_W1 = L2_gnn_W1
    d.L2_gnn_b1 = L2_gnn_b1
    d.L2_gnn_W2 = L2_gnn_W2
    d.L2_gnn_b2 = L2_gnn_b2
    d.L2_gnn_emb = L2_gnn_emb
    d.L2_gnn_adaptW = L2_gnn_adaptW
    d.L2_gnn_gamma = L2_gnn_gamma
    d.L2_gnn_beta = L2_gnn_beta
    d.out = out
    with ExitStack() as ctx:
        ctx.enter_context(nc.allow_non_contiguous_dma(reason="one word per node or chunk"))
        sb = lambda n, shape, dt=F32: ctx.enter_context(nc.sbuf_tensor(n, shape, dt))
        dram = lambda n, shape, dt=F32: nc.dram_tensor(n, shape, dt).ap()
        d.table = dram("table", (NODES, W0))
        d.table_r = dram("table_r", (NODES * RELS, F))
        d.sorted1 = dram("sorted1", (P * ROW1, EDGE))
        d.sorted2 = dram("sorted2", (P * ROW2, MSG))
        d.chunk_tile1 = dram("chunk_tile1", (SLOT_COLS * P * G,), I32)
        d.chunk_tile2 = dram("chunk_tile2", (SLOT_COLS * P * G,), I32)
        d.seg_max = dram("seg_max_rows", (NODES,))
        d.zeros = dram("zeros_rows", (P * U * ATTR,))
        s.x = sb("x", [P, TILES, F])
        s.h = sb("h", [P, TILES, F])
        s.agg = sb("agg", [P, TILES, F + 1])
        s.tab = sb("tab", [P, TILES, W0])
        s.stat = sb("stat", [P, 4, TILES])
        s.nvec = sb("nvec", [P, TILES])
        s.qnode = sb("qnode", [P, TILES, GDIM + 1])
        s.iota = sb("iota", [P, P])
        s.iota_b = sb("iota_b", [P, P], BF16)
        s.ident = sb("ident", [P, P])
        s.ident_b = sb("ident_b", [P, P], BF16)
        s.ones = sb("ones", [P, P])
        s.lower = sb("lower", [P, P])
        s.zeros = sb("zeros", [P, 512])
        s.zeros_b = sb("zeros_b", [P, 512], BF16)
        s.lane = sb("lane", [P, 1])
        s.eps = sb("eps", [P, 1])
        s.half_pi = sb("half_pi", [P, 1])
        s.iota_slot = sb("iota_slot", [P, SLOT_COLS, G])
        s.lane_row = {row: sb(f"lane_row{row}", [P, 1])[:, :] for row in (ROW1, ROW2)}
        s.chunk_tile_i = sb("chunk_tile_i", [P, SLOTS], I32)
        s.source_tile = sb("source_tile", [1, SLOTS], I32)
        s.sentinel2 = sb("sentinel2", [P, SLOTS - FREE_FROM, MSG])
        s.tile_regs = [nc.tensor.alloc_register(f"tile{n}") for n in range(H * G)]
        with ExitStack() as sorting:
            ss = lambda n, shape, dt=F32: sorting.enter_context(nc.sbuf_tensor(n, shape, dt))
            s.sentinel1 = ss("sentinel1", [P, SLOTS - FREE_FROM, EDGE])
            s.meta = ss("meta", [P, CHUNKS, META])
            s.tile_d = ss("tile_d", [P, CHUNKS], BF16)
            setup_phase(nc, s, d)
            with ExitStack() as ranking:
                rb = lambda n, shape, dt=F32: ranking.enter_context(nc.sbuf_tensor("d_" + n, shape, dt))
                ranks = Ranks(rb, ranking.enter_context(nc.psum_tensor("d_rank_ps", [P, 2, BUCKET_COLS], F32)), CHUNKS, ROW1)
                rank_phase(nc, s, d, ranks)
                sort_phase(nc, s, d, ranks.rows)
        s.edge = sb("edge", [P, SLOTS, META])
        s.tile_s = sb("tile_s", [P, SLOTS], BF16)
        s.chunk_tile = sb("chunk_tile", [P, SLOTS])
        s.top = sb("top", [P, SLOTS])
        s.edge_top = sb("edge_top", [P, SLOTS])
        s.adapt = sb("edge_adapt", [P, SLOTS])
        s.mult = sb("mult", [P, SLOTS])
        s.ex = sb("ex", [P, SLOTS])
        s.seg_max = sb("seg_max", [P, TURNS])
        s.max_rows = sb("max_rows", [P, NODES])
        ranks = Ranks(sb, None, SLOTS, ROW2)
        source, related = s.edge[:, :, SRC], s.edge[:, :, REL]
        edge_pass(nc, s, d, "sum1", d.table, W0, F + 1, source, ranks=ranks, find_max=True)
        sage_phase(nc, s, d, "sage1", d.L0_gnn_W_self1, d.L0_gnn_W_neigh1, d.L0_gnn_b1)
        edge_pass(nc, s, d, "sum2", d.table, W0, F + 1, source, ranks=ranks, join_max=True, adapt=True)
        with nc.psum_tensor("s_rank_ps", [P, 2, BUCKET_COLS], F32) as ranks.ps:
            sage_phase(nc, s, d, "sage2", d.L0_gnn_W_self2, d.L0_gnn_W_neigh2, d.L0_gnn_b2, ranks)
        relation_phase(nc, s, d, ranks)
        edge_pass(nc, s, d, "sum3", d.table_r, F, F, related, weight=s.edge[:, :, WEIGHT], ranks=ranks, edge_max=True)
        join_phase(nc, s, d, "join1", "relation", ranks)
        send_pass(nc, s, d, ranks.rows)
        source_pass(nc, s, d)
        join_phase(nc, s, d, "join2", "gated")
        edge_pass(nc, s, d, "sum4", d.table, W0, F + 1, source, weight=s.ex)
        join_phase(nc, s, d, "join3", "softmax")


_INS = ['x', 'src', 'dst', 'edge_attr_40', 'edge_type_8', 'edge_weight', 'edge_weight1', 'node_type_119', 'node_vec',
        'L0_gnn_W_self1', 'L0_gnn_W_neigh1', 'L0_gnn_b1', 'L0_gnn_W_self2', 'L0_gnn_W_neigh2', 'L0_gnn_b2',
        'L1_gnn_weight1', 'L1_gnn_weight2', 'L1_gnn_bias1', 'L1_gnn_bias2',
        'L2_gnn_W1', 'L2_gnn_b1', 'L2_gnn_W2', 'L2_gnn_b2', 'L2_gnn_emb', 'L2_gnn_adaptW', 'L2_gnn_gamma', 'L2_gnn_beta']


def kernel(**inputs):
    import numpy as _np
    import concourse.bacc as _bacc
    from concourse import mybir as _mybir
    from concourse.bass_utils import run_bass_kernel_spmd as _run

    nc = _bacc.Bacc("TRN2", target_bir_lowering=False, num_devices=1)
    arrays, args = {}, {}
    for name in _INS:
        a = _np.ascontiguousarray(inputs[name])
        arrays[f"in_{name}_dram"] = a
        args[name] = nc.dram_tensor(f"in_{name}_dram", a.shape, _mybir.dt.from_np(a.dtype), kind="ExternalInput").ap()
    args["out"] = nc.dram_tensor("out_dram", (N, F), F32, kind="ExternalOutput").ap()
    build(nc, **args)
    r = _run(nc, [arrays], core_ids=[0])
    return r.results[0]["out_dram"]
```
